# Optimizing a Trainium2 kernel written in Bass

```python
import numpy as np
import jax
import jax.numpy as jnp

def _softmax(x, axis=-1):
    return jax.nn.softmax(x, axis=axis)

def _gelu(x):
    return jax.nn.gelu(x, approximate=True)

def _silu(x):
    return jax.nn.silu(x)

def _sigmoid(x):
    return jax.nn.sigmoid(x)

def _layernorm(x, axis=-1, eps=1e-05):
    m = jnp.mean(x, axis=axis, keepdims=True)
    v = jnp.var(x, axis=axis, keepdims=True)
    return (x - m) / jnp.sqrt(v + eps)

def _scatter_add(tgt, idx, src, axis=0):
    return tgt.at[idx].add(src)

def _segment_sum(src, seg, n):
    return jax.ops.segment_sum(src, seg, n)
kernel_name = 'mk_adj_resnorm_d1_adj_r2_7f86a3'

def setup_inputs(seed: int=0):
    np.random.seed(seed)
    _w = jnp.asarray

    def _rec_inputs():
        import jax
        import jax.numpy as jnp
        _gk = jax.random.key(seed)
        x = -0.000929 + 1 * jax.random.normal(jax.random.fold_in(_gk, 1), (4096, 128), jnp.float32)
        _a = jax.random.bernoulli(jax.random.fold_in(_gk, 2), 0.000976562, (4096, 4096))
        _a = jnp.logical_or(_a, jnp.eye(4096, dtype=bool))
        _af = _a.astype(jnp.float32)
        _af = _af * jax.random.uniform(jax.random.fold_in(_gk, 3), (4096, 4096), jnp.float32, 0.05, 1)
        adj = _af
        return (x, adj)
    x, adj = _rec_inputs()

    def _L0_gnn_setup():
        import jax, jax.numpy as jnp
        import numpy as np
        N, H, HEADS = (2048, 128, 3)
        ALPHA = 0.2
        NEG_INF = -9000000000000000.0

        def _sign_adj(key, n, density):
            k1, k2 = jax.random.split(key)
            mask = jax.random.uniform(k1, (n, n)) < density
            sign = jnp.where(jax.random.uniform(k2, (n, n)) < 0.5, -1.0, 1.0)
            adj = jnp.where(mask, sign, 0.0).astype(jnp.float32)
            idx = jnp.arange(n)
            return adj.at[idx, idx].set(1.0)

        def _gru_cell(x, hstate, Wih, Whh, bih, bhh):
            gi = x @ Wih.T + bih
            gh = hstate @ Whh.T + bhh
            ir, iz, inn = jnp.split(gi, 3, axis=1)
            hr, hz, hn = jnp.split(gh, 3, axis=1)
            r = jax.nn.sigmoid(ir + hr)
            z = jax.nn.sigmoid(iz + hz)
            n = jnp.tanh(inn + r * hn)
            return (1.0 - z) * n + z * hstate

        def _gat_head(h, node_adj, edge_adj, W, a):
            hW = h @ W
            hp = (node_adj > 0).astype(hW.dtype) @ hW
            hm = (node_adj < 0).astype(hW.dtype) @ hW
            e_plus = jax.nn.leaky_relu(jnp.concatenate([hp, hm], axis=1) @ a, ALPHA)[:, 0]
            e_minus = jax.nn.leaky_relu(jnp.concatenate([hm, hp], axis=1) @ a, ALPHA)[:, 0]
            att = jnp.where(edge_adj > 0, e_plus[None, :], NEG_INF)
            att = jnp.where(edge_adj < 0, e_minus[None, :], att)
            att = jax.nn.softmax(att, axis=1)
            return att * edge_adj @ hW
        key = jax.random.key(seed)
        ks = jax.random.split(key, 16)
        std = 0.01
        gain = 1.414
        return {'h': jax.random.normal(ks[0], (N, H), jnp.float32), 'node_adj': _sign_adj(ks[1], N, 0.005), 'edge_adj': _sign_adj(ks[2], N, 0.005), 'gat_W': jax.random.normal(ks[3], (HEADS, H, H), jnp.float32) * (gain / np.sqrt(H, dtype=np.float32)), 'gat_a': jax.random.normal(ks[4], (HEADS, 2 * H, 1), jnp.float32) * 0.1, 'edge_Wih': jax.random.normal(ks[5], (3 * H, H), jnp.float32) * std, 'edge_Whh': jax.random.normal(ks[6], (3 * H, H), jnp.float32) * std, 'edge_bih': jnp.zeros((3 * H,), jnp.float32), 'edge_bhh': jnp.zeros((3 * H,), jnp.float32), 'node_Wih': jax.random.normal(ks[7], (3 * H, H), jnp.float32) * std, 'node_Whh': jax.random.normal(ks[8], (3 * H, H), jnp.float32) * std, 'node_bih': jnp.zeros((3 * H,), jnp.float32), 'node_bhh': jnp.zeros((3 * H,), jnp.float32)}
    _L0_gnn_all = _L0_gnn_setup()
    _L0_gnn_in = {k: v for k, v in _L0_gnn_all.items() if k in ('gat_W', 'gat_a', 'edge_Wih', 'edge_Whh', 'edge_bih', 'edge_bhh', 'node_Wih', 'node_Whh', 'node_bih', 'node_bhh')}
    del _L0_gnn_all
    return {'x': x, 'adj': adj, 'L0_gnn_gat_W': _L0_gnn_in['gat_W'], 'L0_gnn_gat_a': _L0_gnn_in['gat_a'], 'L0_gnn_edge_Wih': _L0_gnn_in['edge_Wih'], 'L0_gnn_edge_Whh': _L0_gnn_in['edge_Whh'], 'L0_gnn_edge_bih': _L0_gnn_in['edge_bih'], 'L0_gnn_edge_bhh': _L0_gnn_in['edge_bhh'], 'L0_gnn_node_Wih': _L0_gnn_in['node_Wih'], 'L0_gnn_node_Whh': _L0_gnn_in['node_Whh'], 'L0_gnn_node_bih': _L0_gnn_in['node_bih'], 'L0_gnn_node_bhh': _L0_gnn_in['node_bhh']}

def reference(x, adj, L0_gnn_gat_W, L0_gnn_gat_a, L0_gnn_edge_Wih, L0_gnn_edge_Whh, L0_gnn_edge_bih, L0_gnn_edge_bhh, L0_gnn_node_Wih, L0_gnn_node_Whh, L0_gnn_node_bih, L0_gnn_node_bhh):
    import jax
    import jax.numpy as jnp

    def _L0_gnn_ref(h, node_adj, edge_adj, gat_W, gat_a, edge_Wih, edge_Whh, edge_bih, edge_bhh, node_Wih, node_Whh, node_bih, node_bhh):
        import jax, jax.numpy as jnp
        import numpy as np
        N, H, HEADS = (2048, 128, 3)
        ALPHA = 0.2
        NEG_INF = -9000000000000000.0

        def _sign_adj(key, n, density):
            k1, k2 = jax.random.split(key)
            mask = jax.random.uniform(k1, (n, n)) < density
            sign = jnp.where(jax.random.uniform(k2, (n, n)) < 0.5, -1.0, 1.0)
            adj = jnp.where(mask, sign, 0.0).astype(jnp.float32)
            idx = jnp.arange(n)
            return adj.at[idx, idx].set(1.0)

        def _gru_cell(x, hstate, Wih, Whh, bih, bhh):
            gi = x @ Wih.T + bih
            gh = hstate @ Whh.T + bhh
            ir, iz, inn = jnp.split(gi, 3, axis=1)
            hr, hz, hn = jnp.split(gh, 3, axis=1)
            r = jax.nn.sigmoid(ir + hr)
            z = jax.nn.sigmoid(iz + hz)
            n = jnp.tanh(inn + r * hn)
            return (1.0 - z) * n + z * hstate

        def _gat_head(h, node_adj, edge_adj, W, a):
            hW = h @ W
            hp = (node_adj > 0).astype(hW.dtype) @ hW
            hm = (node_adj < 0).astype(hW.dtype) @ hW
            e_plus = jax.nn.leaky_relu(jnp.concatenate([hp, hm], axis=1) @ a, ALPHA)[:, 0]
            e_minus = jax.nn.leaky_relu(jnp.concatenate([hm, hp], axis=1) @ a, ALPHA)[:, 0]
            att = jnp.where(edge_adj > 0, e_plus[None, :], NEG_INF)
            att = jnp.where(edge_adj < 0, e_minus[None, :], att)
            att = jax.nn.softmax(att, axis=1)
            return att * edge_adj @ hW
        dn = jnp.diag(node_adj)
        de = jnp.diag(edge_adj)
        idx = jnp.arange(node_adj.shape[0])
        node_adj_norm = node_adj.at[idx, idx].add(-dn)
        edge_adj_norm = edge_adj.at[idx, idx].add(-de)
        node_support = node_adj_norm @ h
        edge_output = _gru_cell(node_support, h, edge_Wih, edge_Whh, edge_bih, edge_bhh)
        edge_support = _gat_head(h, node_adj_norm, edge_adj_norm, gat_W[0], gat_a[0])
        for i in range(1, HEADS):
            edge_support = edge_support + _gat_head(h, node_adj_norm, edge_adj_norm, gat_W[i], gat_a[i])
        edge_support = edge_support / HEADS
        node_output = _gru_cell(edge_support, h, node_Wih, node_Whh, node_bih, node_bhh)
        return de[:, None] * edge_output + dn[:, None] * node_output
    x = _layernorm(x + _L0_gnn_ref(x, adj, adj, L0_gnn_gat_W, L0_gnn_gat_a, L0_gnn_edge_Wih, L0_gnn_edge_Whh, L0_gnn_edge_bih, L0_gnn_edge_bhh, L0_gnn_node_Wih, L0_gnn_node_Whh, L0_gnn_node_bih, L0_gnn_node_bhh), axis=-1)
    return x

_drawn_inputs = setup_inputs


def setup_inputs(seed=0):
    import zlib

    import numpy as np

    out = dict(_drawn_inputs(seed))
    spreads = {'L0_gnn_edge_bih': (0.0, 0.402),
     'L0_gnn_edge_bhh': (0.0, 0.685),
     'L0_gnn_node_bih': (0.0, 0.434),
     'L0_gnn_node_bhh': (0.0, 0.667)}
    factors = {'L0_gnn_gat_W': 6.808,
     'L0_gnn_gat_a': 8.0,
     'L0_gnn_edge_Whh': 4.176,
     'L0_gnn_node_Wih': 6.795,
     'L0_gnn_node_Whh': 4.154}
    for name, (base, spread) in spreads.items():
        noise = np.random.default_rng([zlib.crc32(name.encode()), seed]).standard_normal(out[name].shape)
        drawn = base * np.exp(spread * noise) if base else spread * noise
        out[name] = jnp.asarray(drawn.astype(out[name].dtype))
    for name, factor in factors.items():
        out[name] = (out[name] * factor).astype(out[name].dtype)
    return out
```

```python
import numpy as np
from contextlib import ExitStack
import concourse.bass as bass
import concourse.mybir as mybir

P = 128
N = 4096
T = N // P
HEADS = 3
G3 = 3 * P
ALPHA = 0.2
NEG_INF = -9.0e15
EPS = 1e-5

fp32 = mybir.dt.float32
ALU = mybir.AluOpType
ACT = mybir.ActivationFunctionType
AX = mybir.AxisListType


def build(nc, d, out):
    ctx = ExitStack()
    with ctx:
        def sb(name, shape, dt=fp32):
            return ctx.enter_context(nc.sbuf_tensor(name, shape, dt))

        def pb(name, shape, dt=fp32):
            return ctx.enter_context(nc.psum_tensor(name, shape, dt))

        def sem(name):
            return ctx.enter_context(nc.semaphore(name))

        e_dram = nc.dram_tensor("e_rows", (2 * HEADS, N), fp32, kind="Internal").ap()

        X = sb("X", [P, T, P])
        XT = sb("XT", [P, N])
        ST = sb("ST", [P, N])
        NST = sb("NST", [P, N])
        E6 = sb("E6", [P, T, 2 * HEADS])
        diag = sb("diag", [P, T])
        W = sb("W", [P, HEADS, P])
        WT = sb("WT", [P, HEADS, P])
        a12 = sb("a12", [P, 2 * HEADS])
        U = sb("U", [P, 4 * HEADS])
        Wi = sb("Wi", [P, 2, G3])
        Wh = sb("Wh", [P, 2, G3])
        bias = sb("bias", [1, 2, 4 * P])
        braw = sb("braw", [1, 4, G3])
        ones = sb("ones", [P, P])
        ident = sb("ident", [P, P])
        off = sb("off", [P, P])
        eps = sb("eps", [P, 1])

        gA = sb("gA", [P, N])
        gB = sb("gB", [P, N])
        gC = sb("gC", [P, N])
        gEp = sb("gEp", [P, N])
        gEm = sb("gEm", [P, N])
        gW = sb("gW", [P, N])
        gH = sb("gH", [P, 2 * P])
        gN = sb("gN", [P, HEADS, P])
        gmx = sb("gmx", [P, 4])
        gH2 = sb("gH2", [P, 2 * HEADS])

        cur = sb("cur", [P, 3, P])
        th = sb("th", [P, 2, 2 * P])
        nn = sb("nn", [P, 2, P])
        gg = sb("gg", [P, 2, P])
        st6 = sb("st6", [P, 6])
        mv = sb("mv", [P, T, 2])
        mvc = sb("mvc", [P, 2])
        yc = sb("yc", [P, P])
        rstd = sb("rstd", [P, T])
        Y = sb("Y", [P, T, P])

        B = [pb(f"B{i}", [P, 4 * P]) for i in range(6)]
        GRU = pb("GRU", [P, 2, 4 * P])

        s_load = sem("s_load")
        s_c = sem("s_c")
        s_cb = sem("s_cb")
        s_u = sem("s_u")
        s_ue = sem("s_ue")
        block = ctx.enter_context(nc.Block())
        g = {k: sem("g_" + k) for k in (
            "at", "off", "off2", "pm", "mm", "ev", "e", "ed", "eg", "a", "aoff", "ep", "att", "mx",
            "ex", "w", "tr", "cp", "num", "nev", "sup", "sev", "chain")}
        f = {k: sem("f_" + k) for k in ("cur", "gates", "tanh", "pre", "n", "y", "chain", "sq", "rstd", "out", "norm")}
        LOADS = 16 * 11

        @block.sync
        def _(sp):
            with nc.allow_non_contiguous_dma(reason="small"):
                sp.dma_start(X[:, :, :], d["x"].rearrange("(t p) f -> p t f", p=P)).then_inc(s_load, 16)
                sp.dma_start(XT[:, :], d["xT"]).then_inc(s_load, 16)
                sp.dma_start(W[:, :, :], d["gatW"]).then_inc(s_load, 16)
                sp.dma_start(WT[:, :, :], d["gatWT"]).then_inc(s_load, 16)
                sp.dma_start(a12[:, :], d["a12"]).then_inc(s_load, 16)
                sp.dma_start(diag[:, :], d["diag"]).then_inc(s_load, 16)
                sp.dma_start(Wi[:, :, :], d["Wi"]).then_inc(s_load, 16)
                sp.dma_start(Wh[:, :, :], d["Wh"]).then_inc(s_load, 16)
                sp.dma_start(braw[0:1, :, :], d["b"]).then_inc(s_load, 16)
                sp.dma_start(ident[:, :], d["ident"]).then_inc(s_load, 16)
                sp.dma_start(off[:, :], d["off"]).then_inc(s_load, 16)
            adjT = d["adjT"].rearrange("(j p) i -> p j i", p=P)
            with sp.Fori(0, T) as t:
                sp.wait_ge(g["mm"], t + 1)
                sp.dma_start(gA[:, :].rearrange("p (j i) -> p j i", i=P), adjT[:, :, bass.ds(t * P, P)]).then_inc(g["at"], 16)
            sp.wait_ge(g["ed"], T + 1)
            with nc.allow_non_contiguous_dma(reason="the scores as rows"):
                for k in range(2 * HEADS):
                    sp.dma_start(e_dram[k, :].rearrange("(t p) -> p t", p=P), E6[:, :, k]).then_inc(g["eg"], 16)
            sp.wait_ge(g["eg"], 16 * 2 * HEADS)
            with sp.Fori(0, T) as t:
                sp.wait_ge(g["w"], t * HEADS + 1)
                sp.dma_start(gA[:, :], d["adj"][bass.ds(t * P, P), :]).then_inc(g["a"], 16)
                for h in range(HEADS):
                    sp.wait_ge(g["att"], t * HEADS + h + 1)
                    sp.dma_start(gEp[:, :], e_dram[h:h + 1, :].to_broadcast([P, N])).then_inc(g["ep"], 16)
                    sp.dma_start(gEm[:, :], e_dram[HEADS + h:HEADS + h + 1, :].to_broadcast([P, N])).then_inc(g["ep"], 16)
            sp.wait_ge(f["norm"], 1)
            sp.dma_start(out.rearrange("(t p) f -> p t f", p=P), Y[:, :, :]).then_inc(f["out"], 16)
            sp.wait_ge(f["out"], 16)

        @block.gpsimd
        def _(pool):
            nc.gpsimd.memset(ones[:, :], 1.0).then_inc(s_c, 1)
            nc.gpsimd.memset(eps[:, :], EPS).then_inc(s_c, 1)

        def final_pe(pe, i):
            pe.wait_ge(f["cur"], i + 1)
            pe.wait_ge(f["pre"], i + 1)
            for k in range(2):
                ps = GRU[:, k, :]
                nc.tensor.matmul(ps, ones[0:1, :], bias[0:1, k, :], start=True, stop=False)
                nc.tensor.matmul(ps[:, 0:G3], cur[:, k, :], Wi[:, k, :], start=False, stop=False)
                nc.tensor.matmul(ps[:, 0:2 * P], cur[:, 2, :], Wh[:, k, 0:2 * P], start=False, stop=False)
                last = nc.tensor.matmul(ps[:, G3:], cur[:, 2, :], Wh[:, k, 2 * P:], start=False, stop=True)
            last.then_inc(f["gates"], 1)

        def final_act(act, i):
            act.wait_ge(f["gates"], i + 2)
            nc.scalar.activation(th[:, :, :], GRU[:, :, 0:2 * P], ACT.Tanh, scale=0.5).then_inc(f["tanh"], 1)
            act.wait_ge(f["pre"], i + 2)
            nc.scalar.activation(nn[:, :, :], gg[:, :, :], ACT.Tanh).then_inc(f["n"], 1)

        CH = 8

        def final_dve(dve, i):
            xt = X[:, bass.ds(i, 1), :]
            c = [0]

            def link(ins):
                ins.then_inc(f["chain"], 1)
                c[0] += 1
                dve.wait_ge(f["chain"], i * CH + c[0])

            dve.wait_ge(f["tanh"], i + 1)
            link(nc.vector.scalar_tensor_tensor(gg[:, :, :], th[:, :, 0:P], 1.0, GRU[:, :, G3:], ALU.add, ALU.mult))
            nc.vector.scalar_tensor_tensor(gg[:, :, :], gg[:, :, :], 0.5, GRU[:, :, 2 * P:G3], ALU.mult, ALU.add).then_inc(f["pre"], 1)
            dve.wait_ge(f["n"], i + 1)
            link(nc.vector.tensor_tensor(gg[:, :, :], xt.to_broadcast([P, 2, P]), nn[:, :, :], ALU.subtract))
            link(nc.vector.scalar_tensor_tensor(gg[:, :, :], th[:, :, P:], 1.0, gg[:, :, :], ALU.add, ALU.mult))
            link(nc.vector.scalar_tensor_tensor(gg[:, :, :], gg[:, :, :], 0.5, nn[:, :, :], ALU.mult, ALU.add))
            link(nc.vector.tensor_tensor(gg[:, 0, :], gg[:, 0, :], gg[:, 1, :], ALU.add))
            link(nc.vector.scalar_tensor_tensor(yc[:, :], gg[:, 0, :], diag[:, bass.ds(i, 1)],
                                                xt.rearrange("p a f -> p (a f)"), ALU.mult, ALU.add))
            link(nc.vector.bn_stats(st6[:, :], yc[:, :]))
            nc.vector.tensor_copy(Y[:, bass.ds(i, 1), :].rearrange("p a f -> p (a f)"), yc[:, :])
            link(nc.vector.bn_aggr(mvc[:, :], st6[:, :]))
            assert c[0] == CH
            nc.vector.tensor_copy(mv[:, bass.ds(i, 1), :].rearrange("p a f -> p (a f)"), mvc[:, :]).then_inc(f["y"], 1)

        @block.vector
        def _(dve):
            dve.sem_inc(g["w"], 1)
            dve.sem_inc(g["att"], 1)
            dve.sem_inc(f["pre"], 1)
            dve.sem_inc(g["ed"], 1)
            dve.wait_ge(s_load, LOADS)
            c = [0]
            for k in range(2):
                nc.vector.tensor_tensor(bias[0:1, k, 0:2 * P], braw[0:1, 2 * k, 0:2 * P], braw[0:1, 2 * k + 1, 0:2 * P], ALU.add)
                nc.vector.tensor_copy(bias[0:1, k, 2 * P:G3], braw[0:1, 2 * k, 2 * P:])
                last = nc.vector.tensor_copy(bias[0:1, k, G3:], braw[0:1, 2 * k + 1, 2 * P:])
            last.then_inc(s_cb, 1)
            dve.wait_ge(s_u, 1)
            for k, o in ((0, 0), (3, 3), (6, 3), (9, 0)):
                last = nc.vector.tensor_copy(U[:, k:k + 3], B[4][:, o:o + 3])
            last.then_inc(s_ue, 1)
            with dve.Fori(0, T) as t:
                dve.wait_ge(g["at"], 16 * (t + 1))
                blk = gA[:, bass.ds(t * P, P)]
                nc.vector.tensor_tensor(blk, blk, off[:, :], ALU.mult).then_inc(g["off"], 1)
                dve.wait_ge(g["off"], t + 1)
                nc.vector.tensor_scalar(gB[:, :], gA[:, :], 0.0, None, ALU.is_gt)
                nc.vector.tensor_scalar(gC[:, :], gA[:, :], 0.0, None, ALU.is_lt).then_inc(g["pm"], 1)
                dve.wait_ge(g["e"], t + 1)
                nc.vector.tensor_scalar(gH2[:, :], B[4][:, 0:6], ALPHA, None, ALU.mult).then_inc(g["off2"], 1)
                dve.wait_ge(g["off2"], t + 1)
                nc.vector.tensor_tensor(E6[:, bass.ds(t, 1), :].rearrange("p a f -> p (a f)"), B[4][:, 0:6], gH2[:, :], ALU.max).then_inc(g["ed"], 1)
            with dve.Fori(0, T) as t:
                dve.wait_ge(g["a"], 16 * (t + 1))
                blk = gA[:, bass.ds(t * P, P)]
                nc.vector.tensor_tensor(blk, blk, off[:, :], ALU.mult).then_inc(g["aoff"], 1)
                dve.wait_ge(g["aoff"], t + 1)
                for h in range(HEADS):
                    i = t * HEADS + h
                    c = [0]

                    def link(ins):
                        ins.then_inc(g["chain"], 1)
                        c[0] += 1
                        dve.wait_ge(g["chain"], i * 5 + c[0])

                    dve.wait_ge(g["ep"], 32 * (i + 1))
                    dve.wait_ge(g["tr"], 8 * i + 1)
                    link(nc.vector.scalar_tensor_tensor(gB[:, :], gA[:, :], 0.0, gEp[:, :], ALU.is_gt, ALU.mult))
                    link(nc.vector.scalar_tensor_tensor(gC[:, :], gA[:, :], 0.0, gEm[:, :], ALU.is_lt, ALU.mult))
                    nc.vector.tensor_tensor(gB[:, :], gB[:, :], gC[:, :], ALU.add).then_inc(g["att"], 1)
                    dve.wait_ge(g["att"], i + 2)
                    link(nc.vector.tensor_scalar(gC[:, :], gA[:, :], 0.0, NEG_INF, ALU.is_equal, ALU.mult))
                    link(nc.vector.tensor_tensor(gB[:, :], gB[:, :], gC[:, :], ALU.add))
                    nc.vector.tensor_reduce(gmx[:, 1:2], gB[:, :], AX.X, ALU.max, negate=True).then_inc(g["mx"], 1)
                    dve.wait_ge(g["ex"], i + 1)
                    link(nc.vector.reciprocal(gmx[:, 3:4], gmx[:, 2:3]))
                    nc.vector.scalar_tensor_tensor(gB[:, :], gB[:, :], gmx[:, 3:4], gA[:, :], ALU.mult, ALU.mult).then_inc(g["w"], 1)
            with dve.Fori(0, T) as t:
                dve.wait_ge(f["gates"], t + 1)
                dve.wait_ge(g["sev"], T + 1)
                for k, src in enumerate((ST, NST, XT)):
                    last = nc.vector.tensor_copy(cur[:, k, :], src[:, bass.ds(t * P, P)])
                last.then_inc(f["cur"], 1)
                final_dve(dve, t)
            dve.wait_ge(f["sq"], 1)
            nc.vector.reciprocal(rstd[:, :], rstd[:, :]).then_inc(f["rstd"], 1)
            dve.wait_ge(f["rstd"], 1)
            for t in range(T):
                last = nc.vector.tensor_scalar(Y[:, t, :], Y[:, t, :], mv[:, t, 0:1], rstd[:, t:t + 1], ALU.subtract, ALU.mult)
            last.then_inc(f["norm"], 1)

        @block.scalar
        def _(act):
            act.sem_inc(g["ev"], 1)
            act.sem_inc(g["cp"], 1)
            act.sem_inc(g["nev"], 1)
            act.sem_inc(g["sev"], 1)
            with act.Fori(0, T) as t:
                act.wait_ge(g["mm"], t + 2)
                nc.scalar.activation(ST[:, bass.ds(t * P, P)], B[0][:, 0:P], ACT.Copy)
                nc.scalar.activation(gH[:, :], B[0][:, P:G3], ACT.Copy).then_inc(g["ev"], 1)
            with act.Fori(0, T) as t:
                for h in range(HEADS):
                    i = t * HEADS + h
                    act.wait_ge(g["mx"], i + 1)
                    nc.scalar.activation(gB[:, :], gB[:, :], ACT.Exp, bias=gmx[:, 1:2], accum_out=gmx[:, 2:3]).then_inc(g["ex"], 1)
                    for q in range(8):
                        act.wait_ge(g["tr"], 8 * i + q + 2)
                        nc.scalar.activation(gW[:, q * 512:(q + 1) * 512], B[q % 2][:, :], ACT.Copy).then_inc(g["cp"], 1)
                    act.wait_ge(g["num"], i + 1)
                    nc.scalar.activation(gN[:, h, :], B[2][:, 0:P], ACT.Copy).then_inc(g["nev"], 1)
                act.wait_ge(g["sup"], t + 1)
                nc.scalar.activation(NST[:, bass.ds(t * P, P)], B[3][:, 0:P], ACT.Copy, scale=1.0 / HEADS).then_inc(g["sev"], 1)
            with act.Fori(0, T) as t:
                final_act(act, t)
            act.wait_ge(f["y"], T)
            nc.scalar.activation(rstd[:, :], mv[:, :, 1], ACT.Sqrt, bias=eps[:, 0:1]).then_inc(f["sq"], 1)

        @block.tensor
        def _(pe):
            pe.sem_inc(g["mm"], 1)
            pe.sem_inc(f["gates"], 1)
            pe.sem_inc(g["tr"], 1)
            pe.wait_ge(s_load, LOADS)
            pe.wait_ge(s_c, 2)
            for h in range(HEADS):
                for k in range(2):
                    last = nc.tensor.matmul(B[4][:, 3 * k + h:3 * k + h + 1], WT[:, h, :], a12[:, 3 * k + h:3 * k + h + 1], start=True, stop=True)
            last.then_inc(s_u, 1)
            pe.wait_ge(s_ue, 1)
            pe.wait_ge(s_cb, 1)
            with pe.Fori(0, T) as t:
                pe.wait_ge(g["pm"], t + 1)
                pe.wait_ge(g["ev"], t + 1)
                for k, src in enumerate((gA, gB, gC)):
                    for j in range(T):
                        last = nc.tensor.matmul(B[0][:, k * P:(k + 1) * P], X[:, j, :], src[:, j * P:(j + 1) * P], start=(j == 0), stop=(j == T - 1))
                last.then_inc(g["mm"], 1)
                pe.wait_ge(g["ev"], t + 2)
                pe.wait_ge(g["ed"], t + 1)
                nc.tensor.matmul(B[4][:, 0:6], gH[:, 0:P], U[:, 0:6], start=True, stop=False)
                nc.tensor.matmul(B[4][:, 0:6], gH[:, P:], U[:, 6:12], start=False, stop=True).then_inc(g["e"], 1)
            with pe.Fori(0, T) as t:
                for h in range(HEADS):
                    i = t * HEADS + h
                    pe.wait_ge(g["w"], i + 2)
                    for q in range(8):
                        if q < 2:
                            pe.wait_ge(g["cp"], 8 * i + 1)
                        else:
                            pe.wait_ge(g["cp"], 8 * i + q)
                        for j in range(4):
                            last = nc.tensor.transpose(B[q % 2][:, j * P:(j + 1) * P], gB[:, (4 * q + j) * P:(4 * q + j + 1) * P], ident[:, :])
                        last.then_inc(g["tr"], 1)
                    pe.wait_ge(g["cp"], 8 * i + 8 + 1)
                    pe.wait_ge(g["nev"], i + 1)
                    for j in range(T):
                        last = nc.tensor.matmul(B[2][:, 0:P], X[:, j, :], gW[:, j * P:(j + 1) * P], start=(j == 0), stop=(j == T - 1))
                    last.then_inc(g["num"], 1)
                pe.wait_ge(g["nev"], (t + 1) * HEADS + 1)
                pe.wait_ge(g["sev"], t + 1)
                for h in range(HEADS):
                    last = nc.tensor.matmul(B[3][:, 0:P], W[:, h, :], gN[:, h, :], start=(h == 0), stop=(h == HEADS - 1))
                last.then_inc(g["sup"], 1)
            with pe.Fori(0, T) as t:
                final_pe(pe, t)


def kernel(x, adj, L0_gnn_gat_W, L0_gnn_gat_a, L0_gnn_edge_Wih, L0_gnn_edge_Whh, L0_gnn_edge_bih, L0_gnn_edge_bhh,
           L0_gnn_node_Wih, L0_gnn_node_Whh, L0_gnn_node_bih, L0_gnn_node_bhh):
    import concourse.bacc as _bacc
    from concourse.bass_utils import run_bass_kernel_spmd as _run

    c = np.ascontiguousarray
    x, adj = np.asarray(x), np.asarray(adj)
    w, a = np.asarray(L0_gnn_gat_W), np.asarray(L0_gnn_gat_a)
    side = lambda e, n: c(np.stack([np.asarray(e).T, np.asarray(n).T], axis=1))
    arrays = {
        "x": c(x), "xT": c(x.T), "adj": c(adj), "adjT": c(adj.T),
        "diag": c(np.diagonal(adj).reshape(T, P).T),
        "gatW": c(w.transpose(1, 0, 2)), "gatWT": c(w.transpose(2, 0, 1)),
        "a12": c(a.reshape(HEADS, 2, P).transpose(2, 1, 0).reshape(P, 2 * HEADS)),
        "Wi": side(L0_gnn_edge_Wih, L0_gnn_node_Wih), "Wh": side(L0_gnn_edge_Whh, L0_gnn_node_Whh),
        "b": c(np.stack([np.asarray(v) for v in (L0_gnn_edge_bih, L0_gnn_edge_bhh, L0_gnn_node_bih, L0_gnn_node_bhh)])[None]),
        "ident": np.eye(P, dtype=np.float32), "off": 1 - np.eye(P, dtype=np.float32),
    }
    nc = _bacc.Bacc("TRN2", target_bir_lowering=False, num_devices=1)
    d = {k: nc.dram_tensor("in_" + k, v.shape, mybir.dt.from_np(v.dtype), kind="ExternalInput").ap() for k, v in arrays.items()}
    out = nc.dram_tensor("out", (N, P), fp32, kind="ExternalOutput").ap()
    build(nc, d, out)
    r = _run(nc, [{"in_" + k: v for k, v in arrays.items()}], core_ids=[0])
    return r.results[0]["out"]
```

```python
import itertools
import numpy as np
from contextlib import ExitStack
import concourse.bass as bass
import concourse.mybir as mybir

P = 128
N = 4096
T = N // P
HEADS = 3
G3 = 3 * P
ALPHA = 0.2
NEG_INF = -9.0e15
EPS = 1e-5

SLOTS = 16
SEG = N // 4
CAND = 32
GT = 4
NG = T // GT
CH = GT * SLOTS
Q = 32
ROW = P + 4
KEY0 = 128
BIG = 3.0e38

fp32 = mybir.dt.float32
u32 = mybir.dt.uint32
i32 = mybir.dt.int32
bf16 = mybir.dt.bfloat16
ALU = mybir.AluOpType
ACT = mybir.ActivationFunctionType
AX = mybir.AxisListType


def build(nc, d, out):
    ctx = ExitStack()
    with ctx:
        def sb(name, shape, dt=fp32):
            return ctx.enter_context(nc.sbuf_tensor(name, shape, dt))

        def pb(name, shape, dt=fp32):
            return ctx.enter_context(nc.psum_tensor(name, shape, dt))

        def sem(name):
            return ctx.enter_context(nc.semaphore(name))

        e_dram = nc.dram_tensor("e_rows", (2 * HEADS, N), fp32, kind="Internal").ap()

        table = nc.dram_tensor("table", (N + 1, ROW), fp32, kind="Internal").ap()

        TX = sb("TX", [P, T, ROW])
        X = TX[:, :, 0:P]
        XT = sb("XT", [P, N])
        ST = sb("ST", [P, N])
        NST = sb("NST", [P, N])
        Y = NST[:, :].rearrange("p (t f) -> p t f", f=P)
        E6 = sb("E6", [P, T, 2 * HEADS])
        diag = sb("diag", [P, T])
        W = sb("W", [P, HEADS, P])
        WT = sb("WT", [P, HEADS, P])
        a12 = sb("a12", [P, 2 * HEADS])
        U = sb("U", [P, 4 * HEADS])
        Wi = sb("Wi", [P, 2, G3])
        Wh = sb("Wh", [P, 2, G3])
        bias = sb("bias", [1, 2, 4 * P])
        ones = sb("ones", [P, P])
        ident = sb("ident", [P, P])
        off = sb("off", [P, P])
        i32q = sb("i32q", [P, Q])
        seg1 = sb("seg1", [P, GT * CAND])
        dkey = sb("dkey", [P, T])
        eps = sb("eps", [P, 1])

        AV = sb("AV", [P, T, SLOTS])
        MK = sb("MK", [P, T, SLOTS])
        IDX = sb("IDX", [P, NG, CH])
        idx = [sb(f"idx{i}", [P, CH], u32) for i in range(2)]
        cnt = sb("cnt", [P, T])
        zer = sb("zer", [P, T, 2])
        okk = sb("okk", [P, T])
        oks = sb("oks", [P, 2])
        flag = sb("flag", [1, 1], i32)
        V = sb("V", [P, GT, CAND])
        I = sb("I", [P, GT, CAND], u32)
        K = sb("K", [P, GT * CAND])
        K0 = sb("K0", [P, GT * CAND])
        Ks = sb("Ks", [P, GT * CAND], u32)
        KK = sb("KK", [P, 2, GT * CAND], u32)
        KR = sb("KR", [P, 2, GT * CAND])
        S = sb("S", [P, 2, GT, SLOTS])
        Ku = sb("Ku", [P, 2, GT * SLOTS], u32)
        F = sb("F", [P, 2, GT * SLOTS])
        QF = sb("QF", [P, 2, GT * 4, 4])
        HS = sb("HS", [P, 2, P])
        ER = sb("ER", [P, GT * HEADS, SLOTS])
        sm = sb("sm", [P, 3, GT * HEADS])
        MN = sb("MN", [P, GT, SLOTS])
        WQ = sb("WQ", [P, GT * 4, 4, HEADS])
        zrow = sb("zrow", [1, ROW])
        ptick = sb("ptick", [1, 2])
        tick = sb("tick", [P, 128])
        cells = itertools.count()

        def tick_cell():
            n = next(cells)
            return tick[:, n:n + 1]


        arena = sb("arena", [P, 6 * N + 1280])

        def at(start, size):
            assert start + size <= 6 * N + 1280
            return arena[:, start:start + size]

        A = [at(r * N, N) for r in range(4)]
        junk = at(4 * N, N // 4).bitcast(bf16)
        HG1 = [at(4 * N + N // 4 + i * SLOTS * P, SLOTS * P).rearrange("p (c f) -> p c f", f=P) for i in range(2)]
        D1 = [at(5 * N + N // 4 + i * CH * Q, CH * Q).rearrange("p (c q) -> p c q", q=Q) for i in range(2)]
        HG2 = [at(i * CH * ROW, CH * ROW).rearrange("p (c f) -> p c f", f=ROW) for i in range(2)]
        D2 = [at(2 * CH * ROW + i * SLOTS * HEADS * Q, SLOTS * HEADS * Q).rearrange("p (c q) -> p c q", q=Q) for i in range(2)]
        NS = [at(2 * CH * ROW + 2 * SLOTS * HEADS * Q + i * G3, G3).rearrange("p (h i) -> p h i", h=HEADS) for i in range(2)]
        gA, gB, gC, gEp, gEm, gW = (at(k * N, N) for k in range(6))
        gH = at(6 * N, 2 * P)
        gN = at(6 * N + 2 * P, G3).rearrange("p (h i) -> p h i", h=HEADS)
        braw = arena[0:1, 5 * N:5 * N + 4 * G3].rearrange("p (k n) -> p k n", k=4)
        gmx = sb("gmx", [P, 4])
        gH2 = sb("gH2", [P, 2 * HEADS])

        cur = [sb(f"cur{i}", [P, 3, P]) for i in range(2)]
        th = sb("th", [P, 2, 2 * P])
        nn = sb("nn", [P, 2, P])
        gg = sb("gg", [P, 2, P])
        st6 = sb("st6", [P, 6])
        mv = sb("mv", [P, T, 2])
        mvc = sb("mvc", [P, 2])
        yc = sb("yc", [P, P])
        rstd = sb("rstd", [P, T])

        B = [pb(f"B{i}", [P, 4 * P]) for i in range(6)]
        GRU = pb("GRU", [P, 2, 4 * P])

        s_load = sem("s_load")
        s_c = sem("s_c")
        s_cb = sem("s_cb")
        s_u = sem("s_u")
        s_ue = sem("s_ue")
        block = ctx.enter_context(nc.Block())
        g = {k: sem("g_" + k) for k in (
            "at", "off", "off2", "pm", "mm", "ev", "e", "ed", "eg", "a", "aoff", "ep", "att", "mx",
            "ex", "w", "tr", "cp", "num", "nev", "sup", "sev", "chain")}
        f, f2 = ({k: sem(pre + k) for k in ("cur", "gates", "tanh", "pre", "n", "y", "chain", "sq", "rstd", "out", "norm")} for pre in ("f_", "gf_"))
        a_in = [sem(f"a_in{r}") for r in range(4)]
        h_in = [sem(f"h_in{r}") for r in range(2)]
        h2_in = [sem(f"h2_in{r}") for r in range(2)]
        s_max, s_scan, s_chk, s_sel, s_idx, s_mm, s_hev, s_e, s_score, s_zero, s_tab, s_ok, s_okm, s_flag = map(sem, (
            "s_max", "s_scan", "s_chk", "s_sel", "s_idx", "s_mm", "s_hev", "s_e", "s_score", "s_zero", "s_tab", "s_ok", "s_okm", "s_flag"))
        s_half = sem("s_half")
        s_carry = sem("s_carry")
        s_pidx, s_soft, s_ex, s_d2, s_num, s_ns, s_sup = map(sem, (
            "s_pidx", "s_soft", "s_ex", "s_d2", "s_num", "s_ns", "s_sup"))
        LOADS = 16 * 14

        def final_pe(pe, f, i, c):
            pe.wait_ge(f["cur"], i + 2)
            pe.wait_ge(f["pre"], i + 1)
            for k in range(2):
                ps = GRU[:, k, :]
                nc.tensor.matmul(ps, ones[0:1, :], bias[0:1, k, :], start=True, stop=False)
                nc.tensor.matmul(ps[:, 0:G3], c[:, k, :], Wi[:, k, :], start=False, stop=False)
                nc.tensor.matmul(ps[:, 0:2 * P], c[:, 2, :], Wh[:, k, 0:2 * P], start=False, stop=False)
                last = nc.tensor.matmul(ps[:, G3:], c[:, 2, :], Wh[:, k, 2 * P:], start=False, stop=True)
            last.then_inc(f["gates"], 1)

        def final_act(act, f, i):
            act.wait_ge(f["gates"], i + 3)
            act.wait_ge(f["y"], i + 1)
            nc.scalar.activation(th[:, :, :], GRU[:, :, 0:2 * P], ACT.Tanh, scale=0.5).then_inc(f["tanh"], 1)
            act.wait_ge(f["pre"], i + 2)
            nc.scalar.activation(nn[:, :, :], gg[:, :, :], ACT.Tanh).then_inc(f["n"], 1)

        LINKS = 8

        def final_dve(dve, f, i):
            xt = TX[:, bass.ds(i, 1), 0:P]
            c = [0]

            def link(ins):
                ins.then_inc(f["chain"], 1)
                c[0] += 1
                dve.wait_ge(f["chain"], i * LINKS + c[0])

            dve.wait_ge(f["tanh"], i + 1)
            link(nc.vector.scalar_tensor_tensor(gg[:, :, :], th[:, :, 0:P], 1.0, GRU[:, :, G3:], ALU.add, ALU.mult))
            nc.vector.scalar_tensor_tensor(gg[:, :, :], gg[:, :, :], 0.5, GRU[:, :, 2 * P:G3], ALU.mult, ALU.add).then_inc(f["pre"], 1)
            dve.wait_ge(f["n"], i + 1)
            link(nc.vector.tensor_tensor(gg[:, :, :], xt.to_broadcast([P, 2, P]), nn[:, :, :], ALU.subtract))
            link(nc.vector.scalar_tensor_tensor(gg[:, :, :], th[:, :, P:], 1.0, gg[:, :, :], ALU.add, ALU.mult))
            link(nc.vector.scalar_tensor_tensor(gg[:, :, :], gg[:, :, :], 0.5, nn[:, :, :], ALU.mult, ALU.add))
            link(nc.vector.tensor_tensor(gg[:, 0, :], gg[:, 0, :], gg[:, 1, :], ALU.add))
            link(nc.vector.scalar_tensor_tensor(yc[:, :], gg[:, 0, :], diag[:, bass.ds(i, 1)],
                                                xt.rearrange("p a f -> p (a f)"), ALU.mult, ALU.add))
            link(nc.vector.bn_stats(st6[:, :], yc[:, :]))
            nc.vector.memset(tick_cell(), 0.0)
            nc.vector.tensor_copy(Y[:, bass.ds(i, 1), :].rearrange("p a f -> p (a f)"), yc[:, :])
            link(nc.vector.bn_aggr(mvc[:, :], st6[:, :]))
            assert c[0] == LINKS
            nc.vector.tensor_copy(mv[:, bass.ds(i, 1), :].rearrange("p a f -> p (a f)"), mvc[:, :]).then_inc(f["y"], 1)

        PARTS = 4

        def norm_dve(dve, f):
            dve.wait_ge(f["sq"], 1)
            nc.vector.reciprocal(rstd[:, :], rstd[:, :]).then_inc(f["rstd"], 1)
            dve.wait_ge(f["rstd"], 1)
            for t in range(T):
                last = nc.vector.tensor_scalar(Y[:, t, :], Y[:, t, :], mv[:, t, 0:1], rstd[:, t:t + 1], ALU.subtract, ALU.mult)
                if (t + 1) % (T // PARTS) == 0:
                    last.then_inc(f["norm"], 1)

        def norm_act(act, f):
            act.wait_ge(f["y"], T + 1)
            nc.scalar.activation(rstd[:, :], mv[:, :, 1], ACT.Sqrt, bias=eps[:, 0:1]).then_inc(f["sq"], 1)

        def store(sp, f):
            n = T // PARTS
            for k in range(PARTS):
                sp.wait_ge(f["norm"], k + 1)
                sp.dma_start(out.rearrange("(t p) f -> p t f", p=P)[:, k * n:(k + 1) * n, :], Y[:, k * n:(k + 1) * n, :]).then_inc(f["out"], 16)
            sp.wait_ge(f["out"], 16 * PARTS)

        def rest(eng, run):
            eng.wait_ge(s_flag, 1)
            with eng.If(eng.value_load(flag[0:1, 0:1], min_val=0, max_val=1) > 0):
                run()

        @block.sync
        def _(sp):
            with nc.allow_non_contiguous_dma(reason="small"):
                sp.dma_start(TX[:, :, 0:P], d["x1"][1:N + 1, :].rearrange("(t p) f -> p t f", p=P)).then_inc(s_load, 16)
                sp.dma_start(XT[:, :], d["xT"]).then_inc(s_load, 16)
                sp.dma_start(W[:, :, :], d["gatW"]).then_inc(s_load, 16)
                sp.dma_start(WT[:, :, :], d["gatWT"]).then_inc(s_load, 16)
                sp.dma_start(a12[:, :], d["a12"]).then_inc(s_load, 16)
                sp.dma_start(diag[:, :], d["diag"]).then_inc(s_load, 16)
                sp.dma_start(Wi[:, :, :], d["Wi"]).then_inc(s_load, 16)
                sp.dma_start(Wh[:, :, :], d["Wh"]).then_inc(s_load, 16)
                sp.dma_start(braw[0:1, :, :], d["b"]).then_inc(s_load, 16)
                sp.dma_start(ident[:, :], d["ident"]).then_inc(s_load, 16)
                sp.dma_start(i32q[:, :], d["i32q"]).then_inc(s_load, 16)
                sp.dma_start(seg1[:, :], d["seg1"]).then_inc(s_load, 16)
                sp.dma_start(dkey[:, :], d["dkey"]).then_inc(s_load, 16)
                sp.dma_start(off[:, :], d["off"]).then_inc(s_load, 16)
            with sp.Fori(0, NG // 2) as it:
                for u in range(2 * GT):
                    t = it * 2 * GT + u
                    sp.wait_ge(s_scan, t + 1)
                    sp.wait_ge(s_chk, t + 1)
                    sp.dma_start(A[u % 4], d["adj"][bass.ds(t * P, P), :]).then_inc(a_in[u % 4], 16)
            sp.wait_ge(s_zero, 1)
            sp.dma_start(table[0:1, :], zrow[0:1, :]).then_inc(s_tab, 16)
            sp.wait_ge(s_score, 1)
            for k in range(4):
                sp.dma_start(table[1 + k * 8 * P:1 + (k + 1) * 8 * P, :].rearrange("(t p) f -> p t f", p=P), TX[:, k * 8:(k + 1) * 8, :]).then_inc(s_tab, 16)
            store(sp, f)

            def general():
                adjT = d["adjT"].rearrange("(j p) i -> p j i", p=P)
                with sp.Fori(0, T) as t:
                    sp.wait_ge(g["mm"], t + 1)
                    sp.dma_start(gA[:, :].rearrange("p (j i) -> p j i", i=P), adjT[:, :, bass.ds(t * P, P)]).then_inc(g["at"], 16)
                sp.wait_ge(g["ed"], T + 1)
                with nc.allow_non_contiguous_dma(reason="the scores as rows"):
                    for k in range(2 * HEADS):
                        sp.dma_start(e_dram[k, :].rearrange("(t p) -> p t", p=P), E6[:, :, k]).then_inc(g["eg"], 16)
                sp.wait_ge(g["eg"], 16 * 2 * HEADS)
                with sp.Fori(0, T) as t:
                    sp.wait_ge(g["w"], t * HEADS + 1)
                    sp.dma_start(gA[:, :], d["adj"][bass.ds(t * P, P), :]).then_inc(g["a"], 16)
                    for h in range(HEADS):
                        sp.wait_ge(g["att"], t * HEADS + h + 1)
                        sp.dma_start(gEp[:, :], e_dram[h:h + 1, :].to_broadcast([P, N])).then_inc(g["ep"], 16)
                        sp.dma_start(gEm[:, :], e_dram[HEADS + h:HEADS + h + 1, :].to_broadcast([P, N])).then_inc(g["ep"], 16)
                store(sp, f2)

            rest(sp, general)

        @block.gpsimd
        def _(pool):
            nc.gpsimd.memset(ones[:, :], 1.0).then_inc(s_c, 1)
            nc.gpsimd.memset(eps[:, :], EPS).then_inc(s_c, 1)
            nc.gpsimd.memset(TX[:, :, P:], 0.0).then_inc(s_c, 1)
            nc.gpsimd.memset(ptick[:, :], 0.0).then_inc(s_carry, 1)
            nc.gpsimd.memset(zrow[:, :], 0.0).then_inc(s_zero, 1)
            pool.wait_ge(s_zero, 1)
            last_row = pool.to_reg(N)

            def carry(n):
                pool.wait_ge(s_carry, n + 1)
                nc.gpsimd.tensor_tensor(ptick[0:1, 1:2], ptick[0:1, 0:1], ptick[0:1, 0:1], ALU.add).then_inc(s_carry, 1)

            with pool.Fori(0, NG // 2) as it:
                for par in range(2):
                    pool.wait_ge(s_idx, it * 2 + par + 1)
                    for r in range(GT):
                        pool.wait_ge(s_mm, it * 2 * GT + par * GT + r + 7)
                        carry(it * 2 * GT + par * GT + r)
                        for c in range(SLOTS):
                            n = r * SLOTS + c
                            pool.indirect_dma_start(HG1[r % 2][:, c, :], None, d["x1"], bass.IndirectOffsetOnAxis(idx[par][:, n:n + 1], axis=0),
                                                    bounds_check=last_row, oob_is_err=False).then_inc(h_in[r % 2], 16)
            pool.wait_ge(s_mm, T + 8)
            with pool.Fori(0, NG // 2) as it:
                for par in range(2):
                    pool.wait_ge(s_num, it * 2 * GT + par * GT + 4)
                    pool.wait_ge(s_tab, 16 * 5)
                    nc.gpsimd.tensor_copy(idx[par][:, :], IDX[:, bass.ds(it * 2 + par, 1), :].rearrange("p a c -> p (a c)")).then_inc(s_pidx, 1)
                    pool.wait_ge(s_pidx, it * 2 + par + 1)
                    carry(it * 2 + par + T)
                    for n in range(CH):
                        pool.indirect_dma_start(HG2[par][:, n, :], None, table, bass.IndirectOffsetOnAxis(idx[par][:, n:n + 1], axis=0),
                                                bounds_check=last_row, oob_is_err=False).then_inc(h2_in[par], 16)

        @block.vector
        def _(dve):
            dve.sem_inc(g["w"], 1)
            dve.sem_inc(g["att"], 1)
            dve.sem_inc(f["pre"], 1)
            dve.sem_inc(f2["pre"], 1)
            dve.sem_inc(f["y"], 1)
            dve.sem_inc(f2["y"], 1)
            dve.sem_inc(f2["cur"], 1)
            dve.sem_inc(s_scan, 4)
            dve.sem_inc(g["ed"], 1)
            dve.wait_ge(s_load, LOADS)
            c = [0]
            for k in range(2):
                nc.vector.tensor_tensor(bias[0:1, k, 0:2 * P], braw[0:1, 2 * k, 0:2 * P], braw[0:1, 2 * k + 1, 0:2 * P], ALU.add)
                nc.vector.tensor_copy(bias[0:1, k, 2 * P:G3], braw[0:1, 2 * k, 2 * P:])
                last = nc.vector.tensor_copy(bias[0:1, k, G3:], braw[0:1, 2 * k + 1, 2 * P:])
            last.then_inc(s_cb, 1)
            dve.wait_ge(s_u, 1)
            for k, o in ((0, 0), (3, 3), (6, 3), (9, 0)):
                last = nc.vector.tensor_copy(U[:, k:k + 3], B[4][:, o:o + 3])
            last.then_inc(s_ue, 1)

            def chain(sem, base):
                count = [0]

                def done(ins, wait=True):
                    ins.then_inc(sem, 1)
                    count[0] += 1
                    if wait:
                        dve.wait_ge(sem, base + count[0])
                return done, count

            def carry():
                nc.vector.memset(tick_cell(), 0.0)

            SEL = 35

            def select(it, par):
                G = it * 2 + par
                done, count = chain(s_sel, G * SEL)
                flat = lambda x: x.rearrange("p a b -> p (a b)")
                Vf, Vu = flat(V[:, :, :]), flat(V[:, :, :]).bitcast(u32)
                done(nc.vector.tensor_tensor(K0[:, :], flat(I[:, :, :]), seg1[:, :], ALU.add))
                done(nc.vector.scalar_tensor_tensor(K0[:, :], Vf, 0.0, K0[:, :], ALU.is_gt, ALU.mult))
                done(nc.vector.tensor_tensor(K[:, :].rearrange("p (r c) -> p r c", c=CAND), K0[:, :].rearrange("p (r c) -> p r c", c=CAND),
                                             dkey[:, bass.ds(G * GT, GT)].unsqueeze(2).to_broadcast([P, GT, CAND]), ALU.not_equal))
                done(nc.vector.tensor_tensor(K[:, :], K[:, :], K0[:, :], ALU.mult))
                done(nc.vector.tensor_scalar(Ks[:, :], K[:, :], float(KEY0), 65536.0, ALU.add, ALU.mult))
                done(nc.vector.scalar_tensor_tensor(KK[:, 0, :], Vu, 16, Ks[:, :], ALU.logical_shift_right, ALU.bitwise_or), False)
                done(nc.vector.scalar_tensor_tensor(KK[:, 1, :], Vu, 65535, Ks[:, :], ALU.bitwise_and, ALU.bitwise_or))
                KF = KK[:, :, :].bitcast(fp32)
                carry()
                for w in range(2):
                    for r in range(GT):
                        last = nc.vector.max(S[:, w, r, 0:8], KF[:, w, r * CAND:(r + 1) * CAND])
                done(last)
                carry()
                for w in range(2):
                    for r in range(GT):
                        last = nc.vector.match_replace(KR[:, w, r * CAND:(r + 1) * CAND], S[:, w, r, 0:8], KF[:, w, r * CAND:(r + 1) * CAND], 0.0)
                done(last)
                carry()
                for w in range(2):
                    for r in range(GT):
                        last = nc.vector.max(S[:, w, r, 8:16], KR[:, w, r * CAND:(r + 1) * CAND])
                done(last)
                S1, S2 = (S[:, w, :, :].rearrange("p r s -> p (r s)").bitcast(u32) for w in range(2))
                done(nc.vector.tensor_scalar(Ku[:, 0, :], S1, 16, None, ALU.logical_shift_right), False)
                done(nc.vector.tensor_scalar(Ku[:, 1, :], S2, 65535, None, ALU.bitwise_and))
                done(nc.vector.scalar_tensor_tensor(Ku[:, 1, :], S1, 16, Ku[:, 1, :], ALU.logical_shift_left, ALU.bitwise_or), False)
                done(nc.vector.tensor_scalar(F[:, 0, :], Ku[:, 0, :], float(KEY0), None, ALU.subtract))
                done(nc.vector.scalar_tensor_tensor(F[:, 1, :], F[:, 0, :], 0.0, Ku[:, 1, :].bitcast(fp32), ALU.is_gt, ALU.mult))
                mk = MK[:, bass.ds(G * GT, GT), :]
                done(nc.vector.tensor_scalar(mk, F[:, 0, :].rearrange("p (r s) -> p r s", s=SLOTS), 0.0, None, ALU.is_gt))
                done(nc.vector.tensor_copy(AV[:, bass.ds(G * GT, GT), :], F[:, 1, :].rearrange("p (r s) -> p r s", s=SLOTS)), False)
                done(nc.vector.tensor_reduce(cnt[:, bass.ds(G * GT, GT)], mk, AX.X, ALU.add), False)
                for q in range(4):
                    for b in range(4):
                        done(nc.vector.tensor_copy(QF[Q * q:Q * (q + 1), :, :, b],
                                                   F[Q * b:Q * (b + 1), :, :].rearrange("p w (k q) -> p w k q", q=4)[:, :, :, q]), q == 3 and b == 3)
                dve.wait_ge(s_mm, it * 2 * GT + par * GT + 4)
                keys = QF[:, 0, :, :].rearrange("p k b -> p (k b)")
                vals = QF[:, 1, :, :].rearrange("p k b -> p (k b)")
                carry()
                done(nc.vector.tensor_copy(IDX[:, bass.ds(G, 1), :].rearrange("p a c -> p (a c)"), keys), False)
                nc.vector.tensor_copy(idx[par][:, :], keys)
                nc.vector.tensor_tensor(D1[par], vals.unsqueeze(2).to_broadcast([P, CH, Q]), i32q[:, :].unsqueeze(1).to_broadcast([P, CH, Q]), ALU.mult).then_inc(s_idx, 1)
                assert count[0] == SEL, count[0]

            with dve.Fori(0, NG // 2) as it:
                for par in range(2):
                    for r in range(GT):
                        t = it * 2 * GT + par * GT + r
                        dve.wait_ge(a_in[r], 16 * (it * 2 + par + 1))
                        carry()
                        for s in range(4):
                            last = nc.vector.max(V[:, r, 8 * s:8 * s + 8], A[r][:, s * SEG:(s + 1) * SEG])
                        last.then_inc(s_max, 1)
                        dve.wait_ge(s_max, t + 1)
                        carry()
                        for s in range(4):
                            last = nc.vector.max_index(I[:, r, 8 * s:8 * s + 8], V[:, r, 8 * s:8 * s + 8], A[r][:, s * SEG:(s + 1) * SEG])
                        last.then_inc(s_scan, 1)
                    dve.wait_ge(s_scan, it * 2 * GT + (par + 1) * GT + 4)
                    select(it, par)
            dve.wait_ge(s_chk, T + 4)
            done, count = chain(s_ok, 0)
            done(nc.vector.tensor_tensor(okk[:, :], zer[:, :, 0], zer[:, :, 1], ALU.add))
            done(nc.vector.tensor_tensor(okk[:, :], okk[:, :], cnt[:, :], ALU.add))
            done(nc.vector.scalar_tensor_tensor(okk[:, :], diag[:, :], 0.0, okk[:, :], ALU.not_equal, ALU.add))
            done(nc.vector.tensor_scalar(mv[:, :, 0], okk[:, :], N - 0.5, None, ALU.is_gt))
            done(nc.vector.scalar_tensor_tensor(okk[:, :], okk[:, :], N + 0.5, mv[:, :, 0], ALU.is_lt, ALU.mult))
            nc.vector.tensor_reduce(oks[:, 0:1], okk[:, :], AX.X, ALU.add).then_inc(s_okm, 1)
            dve.wait_ge(s_okm, 2)
            nc.vector.tensor_scalar(flag[0:1, 0:1], B[5][0:1, 0:1], N - 0.5, None, ALU.is_lt).then_inc(s_flag, 1)
            dve.wait_ge(s_e, T)
            EB = B[4][:, 0:T * HEADS].rearrange("p (t h) -> p t h", h=HEADS)
            done(nc.vector.tensor_scalar(E6[:, :, 0:HEADS], EB, ALPHA, None, ALU.mult))
            nc.vector.tensor_tensor(TX[:, :, P:P + HEADS], E6[:, :, 0:HEADS], EB, ALU.max).then_inc(s_score, 1)
            dve.wait_ge(s_score, 1)

            SOFT = 41

            def softmax(it, par):
                G = it * 2 + par
                done, count = chain(s_soft, G * SOFT)
                dve.wait_ge(h2_in[par], 16 * CH * (it + 1))
                H = HG2[par].rearrange("p (k b) f -> p k b f", b=4)
                W4 = lambda x: x[:, :, :].rearrange("p (r h) s -> p r h s", h=HEADS)
                for q in range(4):
                    for b in range(4):
                        o = ER[Q * b:Q * (b + 1), :, :].rearrange("p (r h) (k q) -> p r k h q", h=HEADS, q=4)[:, :, :, :, q]
                        i_ = H[Q * q:Q * (q + 1), :, b, P:P + HEADS].rearrange("p (r k) h -> p r k h", k=4)
                        done(nc.vector.tensor_copy(o, i_), False)
                mk = MK[:, bass.ds(G * GT, GT), :]
                av = AV[:, bass.ds(G * GT, GT), :]
                bc = lambda x: x.unsqueeze(2).to_broadcast([P, GT, HEADS, SLOTS])
                done(nc.vector.tensor_scalar(MN[:, :, :], mk, 1.0, -NEG_INF, ALU.subtract, ALU.mult))
                done(nc.vector.tensor_tensor(W4(ER), W4(ER), bc(mk), ALU.mult))
                done(nc.vector.tensor_tensor(W4(ER), W4(ER), bc(MN[:, :, :]), ALU.add))
                done(nc.vector.tensor_reduce(sm[:, 0, :], ER[:, :, :], AX.X, ALU.max))
                done(nc.vector.tensor_tensor(ER[:, :, :], ER[:, :, :], sm[:, 0, :].unsqueeze(2).to_broadcast([P, GT * HEADS, SLOTS]), ALU.subtract))
                nc.vector.memset(tick_cell(), 0.0).then_inc(s_ex, 1)
                dve.wait_ge(s_ex, 2 * G + 2)
                done(nc.vector.tensor_reduce(sm[:, 1, :], ER[:, :, :], AX.X, ALU.add))
                done(nc.vector.tensor_tensor(W4(ER), W4(ER), bc(av), ALU.mult))
                done(nc.vector.reciprocal(sm[:, 2, :], sm[:, 1, :]))
                done(nc.vector.tensor_tensor(ER[:, :, :], ER[:, :, :], sm[:, 2, :].unsqueeze(2).to_broadcast([P, GT * HEADS, SLOTS]), ALU.mult))
                for q in range(4):
                    for b in range(4):
                        i_ = ER[Q * b:Q * (b + 1), :, :].rearrange("p (r h) (k q) -> p r k h q", h=HEADS, q=4)[:, :, :, :, q]
                        o = WQ[Q * q:Q * (q + 1), :, b, :].rearrange("p (r k) h -> p r k h", k=4)
                        done(nc.vector.tensor_copy(o, i_), q == 3 and b == 3)
                assert count[0] == SOFT, count[0]

            def spread(t, r):
                dve.wait_ge(s_num, t + 7)
                n = SLOTS * HEADS
                w = WQ[:, r * 4:(r + 1) * 4, :, :].rearrange("p k b h -> p (k b h)")
                nc.vector.tensor_tensor(D2[r % 2], w.unsqueeze(2).to_broadcast([P, n, Q]),
                                        i32q[:, :].unsqueeze(1).to_broadcast([P, n, Q]), ALU.mult).then_inc(s_d2, 1)

            with dve.Fori(0, NG // 2) as it:
                for par in range(2):
                    t = it * 2 * GT + par * GT
                    softmax(it, par)
                    spread(t, 0)
                    for r in range(GT):
                        if r + 1 < GT:
                            spread(t + r + 1, r + 1)
                        final_dve(dve, f, t + r)
            norm_dve(dve, f)

            def general():
                dve.wait_ge(f["out"], 16 * PARTS)
                with dve.Fori(0, T) as t:
                    dve.wait_ge(g["at"], 16 * (t + 1))
                    blk = gA[:, bass.ds(t * P, P)]
                    nc.vector.tensor_tensor(blk, blk, off[:, :], ALU.mult).then_inc(g["off"], 1)
                    dve.wait_ge(g["off"], t + 1)
                    nc.vector.tensor_scalar(gB[:, :], gA[:, :], 0.0, None, ALU.is_gt)
                    nc.vector.tensor_scalar(gC[:, :], gA[:, :], 0.0, None, ALU.is_lt).then_inc(g["pm"], 1)
                    dve.wait_ge(g["e"], t + 1)
                    nc.vector.tensor_scalar(gH2[:, :], B[4][:, 0:6], ALPHA, None, ALU.mult).then_inc(g["off2"], 1)
                    dve.wait_ge(g["off2"], t + 1)
                    nc.vector.tensor_tensor(E6[:, bass.ds(t, 1), :].rearrange("p a f -> p (a f)"), B[4][:, 0:6], gH2[:, :], ALU.max).then_inc(g["ed"], 1)
                with dve.Fori(0, T) as t:
                    dve.wait_ge(g["a"], 16 * (t + 1))
                    blk = gA[:, bass.ds(t * P, P)]
                    nc.vector.tensor_tensor(blk, blk, off[:, :], ALU.mult).then_inc(g["aoff"], 1)
                    dve.wait_ge(g["aoff"], t + 1)
                    for h in range(HEADS):
                        i = t * HEADS + h
                        c = [0]

                        def link(ins):
                            ins.then_inc(g["chain"], 1)
                            c[0] += 1
                            dve.wait_ge(g["chain"], i * 5 + c[0])

                        dve.wait_ge(g["ep"], 32 * (i + 1))
                        dve.wait_ge(g["tr"], 8 * i + 1)
                        link(nc.vector.scalar_tensor_tensor(gB[:, :], gA[:, :], 0.0, gEp[:, :], ALU.is_gt, ALU.mult))
                        link(nc.vector.scalar_tensor_tensor(gC[:, :], gA[:, :], 0.0, gEm[:, :], ALU.is_lt, ALU.mult))
                        nc.vector.tensor_tensor(gB[:, :], gB[:, :], gC[:, :], ALU.add).then_inc(g["att"], 1)
                        dve.wait_ge(g["att"], i + 2)
                        link(nc.vector.tensor_scalar(gC[:, :], gA[:, :], 0.0, NEG_INF, ALU.is_equal, ALU.mult))
                        link(nc.vector.tensor_tensor(gB[:, :], gB[:, :], gC[:, :], ALU.add))
                        nc.vector.tensor_reduce(gmx[:, 1:2], gB[:, :], AX.X, ALU.max, negate=True).then_inc(g["mx"], 1)
                        dve.wait_ge(g["ex"], i + 1)
                        link(nc.vector.reciprocal(gmx[:, 3:4], gmx[:, 2:3]))
                        nc.vector.scalar_tensor_tensor(gB[:, :], gB[:, :], gmx[:, 3:4], gA[:, :], ALU.mult, ALU.mult).then_inc(g["w"], 1)
                with dve.Fori(0, T) as t:
                    dve.wait_ge(f2["gates"], t + 2)
                    dve.wait_ge(g["sev"], T + 1)
                    for k, src in enumerate((ST, NST, XT)):
                        last = nc.vector.tensor_copy(cur[0][:, k, :], src[:, bass.ds(t * P, P)])
                    last.then_inc(f2["cur"], 1)
                    final_dve(dve, f2, t)
                norm_dve(dve, f2)

            rest(dve, general)

        @block.scalar
        def _(act):
            act.sem_inc(g["ev"], 1)
            act.sem_inc(g["cp"], 1)
            act.sem_inc(g["nev"], 1)
            act.sem_inc(g["sev"], 1)
            act.sem_inc(s_chk, 4)
            act.sem_inc(s_hev, 2)
            act.sem_inc(s_ns, 2)
            act.sem_inc(f["cur"], 1)

            def count_zeros(t, r):
                act.wait_ge(s_chk, t + 4)
                for k in range(2):
                    if k == 1:
                        act.wait_ge(s_half, t + 1)
                    last = nc.scalar.activation(junk, A[r][:, k * N // 2:(k + 1) * N // 2], ACT.Exp, scale=-BIG,
                                                accum_out=zer[:, bass.ds(t, 1), k:k + 1].rearrange("p a b -> p (a b)"))
                    if k == 0:
                        last.then_inc(s_half, 1)
                last.then_inc(s_chk, 1)

            def evict(t, r):
                act.wait_ge(s_mm, t + 9)
                nc.scalar.activation(ST[:, bass.ds(t * P, P)], B[2 * (r % 2)][:, 0:P], ACT.Copy)
                nc.scalar.activation(HS[:, r % 2, :], B[2 * (r % 2) + 1][:, 0:P], ACT.Copy).then_inc(s_hev, 1)

            for r in range(GT):
                act.wait_ge(a_in[r], 16)
                count_zeros(r, r)
            with act.Fori(0, NG // 2 - 1) as it:
                for par in range(2):
                    for r in range(GT):
                        t = it * 2 * GT + par * GT + r
                        act.wait_ge(a_in[r], 16 * (it * 2 + par + 2))
                        count_zeros(t + GT, r)
                        evict(t, r)
            for r in range(GT):
                t = T - 2 * GT + r
                act.wait_ge(a_in[r], 16 * NG)
                count_zeros(t + GT, r)
                evict(t, r)
            for r in range(GT):
                evict(T - GT + r, r)

            def begin(t, r):
                act.wait_ge(f["gates"], t + 1)
                nc.scalar.activation(cur[r % 2][:, 0, :], ST[:, bass.ds(t * P, P)], ACT.Copy)
                nc.scalar.activation(cur[r % 2][:, 2, :], XT[:, bass.ds(t * P, P)], ACT.Copy)
                act.wait_ge(s_num, t + 9)
                nc.scalar.activation(NS[r % 2].rearrange("p h (b i) -> p b h i", i=Q), B[r % 2][:, 0:G3].rearrange("p (b h i) -> p b h i", h=HEADS, i=Q),
                                     ACT.Copy).then_inc(s_ns, 1)

            with act.Fori(0, NG // 2) as it:
                for par in range(2):
                    G = it * 2 + par
                    act.wait_ge(s_ex, 2 * G + 1)
                    nc.scalar.activation(ER[:, :, :], ER[:, :, :], ACT.Exp).then_inc(s_ex, 1)
                    t = it * 2 * GT + par * GT
                    begin(t, 0)
                    for r in range(GT):
                        if r + 1 < GT:
                            begin(t + r + 1, r + 1)
                        act.wait_ge(s_sup, t + r + 1)
                        nc.scalar.activation(cur[r % 2][:, 1, :], B[2][:, 0:P], ACT.Copy, scale=1.0 / HEADS).then_inc(f["cur"], 1)
                        final_act(act, f, t + r)
            norm_act(act, f)

            def general():
                with act.Fori(0, T) as t:
                    act.wait_ge(g["mm"], t + 2)
                    nc.scalar.activation(ST[:, bass.ds(t * P, P)], B[0][:, 0:P], ACT.Copy)
                    nc.scalar.activation(gH[:, :], B[0][:, P:G3], ACT.Copy).then_inc(g["ev"], 1)
                with act.Fori(0, T) as t:
                    for h in range(HEADS):
                        i = t * HEADS + h
                        act.wait_ge(g["mx"], i + 1)
                        nc.scalar.activation(gB[:, :], gB[:, :], ACT.Exp, bias=gmx[:, 1:2], accum_out=gmx[:, 2:3]).then_inc(g["ex"], 1)
                        for q in range(8):
                            act.wait_ge(g["tr"], 8 * i + q + 2)
                            nc.scalar.activation(gW[:, q * 512:(q + 1) * 512], B[q % 2][:, :], ACT.Copy).then_inc(g["cp"], 1)
                        act.wait_ge(g["num"], i + 1)
                        nc.scalar.activation(gN[:, h, :], B[2][:, 0:P], ACT.Copy).then_inc(g["nev"], 1)
                    act.wait_ge(g["sup"], t + 1)
                    nc.scalar.activation(NST[:, bass.ds(t * P, P)], B[3][:, 0:P], ACT.Copy, scale=1.0 / HEADS).then_inc(g["sev"], 1)
                with act.Fori(0, T) as t:
                    final_act(act, f2, t)
                norm_act(act, f2)

            rest(act, general)

        @block.tensor
        def _(pe):
            pe.sem_inc(g["mm"], 1)
            pe.sem_inc(f["gates"], 2)
            pe.sem_inc(f2["gates"], 2)
            pe.sem_inc(s_mm, 8)
            pe.sem_inc(s_num, 8)
            pe.sem_inc(g["tr"], 1)
            pe.wait_ge(s_load, LOADS)
            pe.wait_ge(s_c, 3)
            for h in range(HEADS):
                for k in range(2):
                    last = nc.tensor.matmul(B[4][:, 3 * k + h:3 * k + h + 1], WT[:, h, :], a12[:, 3 * k + h:3 * k + h + 1], start=True, stop=True)
            last.then_inc(s_u, 1)
            pe.wait_ge(s_ue, 1)
            pe.wait_ge(s_cb, 1)

            with pe.Fori(0, NG // 2) as it:
                for par in range(2):
                    pe.wait_ge(s_idx, it * 2 + par + 1)
                    for r in range(GT):
                        t = it * 2 * GT + par * GT + r
                        pe.wait_ge(h_in[r % 2], 16 * SLOTS * (it * 4 + par * 2 + r // 2 + 1))
                        pe.wait_ge(s_hev, t + 1)
                        for w in range(2):
                            for b in range(4):
                                for k in range(4):
                                    c = 4 * k + b
                                    rhs = D1[par][:, r * SLOTS + c, :] if w == 0 else i32q[:, :]
                                    last = nc.tensor.matmul(B[2 * (r % 2) + w][:, b * Q:(b + 1) * Q], HG1[r % 2][:, c, :], rhs, start=(k == 0), stop=(k == 3))
                        last.then_inc(s_mm, 1)
                        pe.wait_ge(s_hev, t + 3)
                        nc.tensor.matmul(B[4][:, bass.ds(t * HEADS, HEADS)], HS[:, r % 2, :], U[:, 0:HEADS], start=True, stop=True).then_inc(s_e, 1)
            pe.wait_ge(s_okm, 1)
            nc.tensor.matmul(B[5][0:1, 0:1], oks[:, 0:1], ones[:, 0:1], start=True, stop=True).then_inc(s_okm, 1)

            def heads(t, r):
                pe.wait_ge(s_d2, t + 1)
                pe.wait_ge(s_ns, t + 1)
                for b in range(4):
                    for k in range(4):
                        c = 4 * k + b
                        last = nc.tensor.matmul(B[r % 2][:, b * HEADS * Q:(b + 1) * HEADS * Q], HGr(r, c), D2c(r, c), start=(k == 0), stop=(k == 3))
                last.then_inc(s_num, 1)

            with pe.Fori(0, NG // 2) as it:
                for par in range(2):
                    HGr = lambda r, c: HG2[par][:, r * SLOTS + c, 0:P]
                    D2c = lambda r, c: D2[r % 2][:, c * HEADS:(c + 1) * HEADS, :].rearrange("p h q -> p (h q)")
                    t = it * 2 * GT + par * GT
                    heads(t, 0)
                    for r in range(GT):
                        if r + 1 < GT:
                            heads(t + r + 1, r + 1)
                        pe.wait_ge(s_ns, t + r + 3)
                        pe.wait_ge(f["cur"], t + r + 1)
                        for h in range(HEADS):
                            last = nc.tensor.matmul(B[2][:, 0:P], W[:, h, :], NS[r % 2][:, h, :], start=(h == 0), stop=(h == HEADS - 1))
                        last.then_inc(s_sup, 1)
                        final_pe(pe, f, t + r, cur[r % 2])

            def general():
                with pe.Fori(0, T) as t:
                    pe.wait_ge(g["pm"], t + 1)
                    pe.wait_ge(g["ev"], t + 1)
                    for k, src in enumerate((gA, gB, gC)):
                        for j in range(T):
                            last = nc.tensor.matmul(B[0][:, k * P:(k + 1) * P], X[:, j, :], src[:, j * P:(j + 1) * P], start=(j == 0), stop=(j == T - 1))
                    last.then_inc(g["mm"], 1)
                    pe.wait_ge(g["ev"], t + 2)
                    pe.wait_ge(g["ed"], t + 1)
                    nc.tensor.matmul(B[4][:, 0:6], gH[:, 0:P], U[:, 0:6], start=True, stop=False)
                    nc.tensor.matmul(B[4][:, 0:6], gH[:, P:], U[:, 6:12], start=False, stop=True).then_inc(g["e"], 1)
                with pe.Fori(0, T) as t:
                    for h in range(HEADS):
                        i = t * HEADS + h
                        pe.wait_ge(g["w"], i + 2)
                        for q in range(8):
                            if q < 2:
                                pe.wait_ge(g["cp"], 8 * i + 1)
                            else:
                                pe.wait_ge(g["cp"], 8 * i + q)
                            for j in range(4):
                                last = nc.tensor.transpose(B[q % 2][:, j * P:(j + 1) * P], gB[:, (4 * q + j) * P:(4 * q + j + 1) * P], ident[:, :])
                            last.then_inc(g["tr"], 1)
                        pe.wait_ge(g["cp"], 8 * i + 8 + 1)
                        pe.wait_ge(g["nev"], i + 1)
                        for j in range(T):
                            last = nc.tensor.matmul(B[2][:, 0:P], X[:, j, :], gW[:, j * P:(j + 1) * P], start=(j == 0), stop=(j == T - 1))
                        last.then_inc(g["num"], 1)
                    pe.wait_ge(g["nev"], (t + 1) * HEADS + 1)
                    pe.wait_ge(g["sev"], t + 1)
                    for h in range(HEADS):
                        last = nc.tensor.matmul(B[3][:, 0:P], W[:, h, :], gN[:, h, :], start=(h == 0), stop=(h == HEADS - 1))
                    last.then_inc(g["sup"], 1)
                with pe.Fori(0, T) as t:
                    final_pe(pe, f2, t, cur[0])

            rest(pe, general)


def kernel(x, adj, L0_gnn_gat_W, L0_gnn_gat_a, L0_gnn_edge_Wih, L0_gnn_edge_Whh, L0_gnn_edge_bih, L0_gnn_edge_bhh,
           L0_gnn_node_Wih, L0_gnn_node_Whh, L0_gnn_node_bih, L0_gnn_node_bhh):
    import concourse.bacc as _bacc
    from concourse.bass_utils import run_bass_kernel_spmd as _run

    c = np.ascontiguousarray
    x, adj = np.asarray(x), np.asarray(adj)
    w, a = np.asarray(L0_gnn_gat_W), np.asarray(L0_gnn_gat_a)
    side = lambda e, n: c(np.stack([np.asarray(e).T, np.asarray(n).T], axis=1))
    arrays = {
        "x1": np.concatenate([np.zeros((1, P), np.float32), x]), "xT": c(x.T), "adj": c(adj), "adjT": c(adj.T),
        "diag": c(np.diagonal(adj).reshape(T, P).T),
        "gatW": c(w.transpose(1, 0, 2)), "gatWT": c(w.transpose(2, 0, 1)),
        "a12": c(a.reshape(HEADS, 2, P).transpose(2, 1, 0).reshape(P, 2 * HEADS)),
        "Wi": side(L0_gnn_edge_Wih, L0_gnn_node_Wih), "Wh": side(L0_gnn_edge_Whh, L0_gnn_node_Whh),
        "b": c(np.stack([np.asarray(v) for v in (L0_gnn_edge_bih, L0_gnn_edge_bhh, L0_gnn_node_bih, L0_gnn_node_bhh)])[None]),
        "ident": np.eye(P, dtype=np.float32), "off": 1 - np.eye(P, dtype=np.float32),
        "i32q": np.tile(np.eye(Q, dtype=np.float32), (4, 1)),
        "seg1": np.tile(np.repeat(np.arange(4, dtype=np.float32) * SEG + 1, 8), (P, GT)),
        "dkey": np.arange(1, N + 1, dtype=np.float32).reshape(T, P).T.copy(),
    }
    nc = _bacc.Bacc("TRN2", target_bir_lowering=False, num_devices=1)
    d = {k: nc.dram_tensor("in_" + k, v.shape, mybir.dt.from_np(v.dtype), kind="ExternalInput").ap() for k, v in arrays.items()}
    out = nc.dram_tensor("out", (N, P), fp32, kind="ExternalOutput").ap()
    build(nc, d, out)
    r = _run(nc, [{"in_" + k: v for k, v in arrays.items()}], core_ids=[0])
    return r.results[0]["out"]
```

```python
import itertools
import numpy as np
from contextlib import ExitStack
import concourse.bass as bass
import concourse.mybir as mybir

P = 128
N = 4096
T = N // P
HEADS = 3
G3 = 3 * P
ALPHA = 0.2
NEG_INF = -9.0e15
EPS = 1e-5

KC = 9
SLOTS = 4 * KC
RND = 5
SEG = N // 4
CAND = 32
GT = 4
NG = T // GT
CH = GT * KC
Q = 32
GP = GT * P
ROW = P + 4
KEY0 = 128

fp32 = mybir.dt.float32
u32 = mybir.dt.uint32
i32 = mybir.dt.int32
ALU = mybir.AluOpType
ACT = mybir.ActivationFunctionType
AX = mybir.AxisListType



def build(nc, d, out):
    ctx = ExitStack()
    with ctx:
        def sb(name, shape, dt=fp32):
            return ctx.enter_context(nc.sbuf_tensor(name, shape, dt))

        def pb(name, shape, dt=fp32):
            return ctx.enter_context(nc.psum_tensor(name, shape, dt))

        def sem(name):
            return ctx.enter_context(nc.semaphore(name))

        e_dram = nc.dram_tensor("e_rows", (2 * HEADS, N), fp32, kind="Internal").ap()

        table = nc.dram_tensor("table", (N + 1, ROW), fp32, kind="Internal").ap()

        TX = sb("TX", [P, T, ROW])
        X = TX[:, :, 0:P]
        ST = sb("ST", [P, N])
        NST = sb("NST", [P, N])
        E6 = sb("E6", [P, T, 2 * HEADS])
        diag = sb("diag", [P, T])
        W = sb("W", [P, HEADS, P])
        WT = sb("WT", [P, HEADS, P])
        a12 = sb("a12", [P, 2 * HEADS])
        U = sb("U", [P, 4 * HEADS])
        Wi = sb("Wi", [P, 2, G3])
        Wh = sb("Wh", [P, 2, G3])
        bT = sb("bT", [P, 4, 3])
        gb = sb("gb", [P, 2, 4])
        ones = sb("ones", [P, P])
        iota = sb("iota", [P, P])
        ident = sb("ident", [P, P])
        half = sb("half", [P, 1])
        rq = sb("rq", [P, 1])
        bounds = sb("bounds", [P, 2, 4])
        seg1 = sb("seg1", [P, GT * CAND])
        dkey = sb("dkey", [P, T])
        eps = sb("eps", [P, 1])

        AV = sb("AV", [P, NG, SLOTS])
        MB = sb("MB", [P, NG, 4, SLOTS])
        IDX = sb("IDX", [P, NG, CH])
        TG = sb("TG", [P, NG, CH])
        idx = [sb(f"idx{i}", [P, CH], u32) for i in range(2)]
        vQ = [sb(f"vQ{i}", [P, CH]) for i in range(2)]
        sgn = sb("sgn", [P, T, 2])
        chk = sb("chk", [P, 6])
        flag = sb("flag", [1, 1], i32)
        V = sb("V", [P, GT, CAND])
        I = sb("I", [P, GT, CAND], u32)
        K = sb("K", [P, GT * CAND])
        K0 = sb("K0", [P, GT * CAND])
        Ks = sb("Ks", [P, GT * CAND], u32)
        KK = sb("KK", [P, 2, GT * CAND], u32)
        QK = sb("QK", [P, 2, 2, 4, CAND])
        S = sb("S", [P, 2, 8 * RND])
        Ku = sb("Ku", [P, 2, SLOTS], u32)
        F = sb("F", [P, 4, SLOTS])
        MH = sb("MH", [P, 4, SLOTS])
        QF = sb("QF", [P, 3, GT, KC])
        HS = sb("HS", [P, 2, P])
        EQ = sb("EQ", [P, HEADS, SLOTS])
        ER = sb("ER", [P, 4 * HEADS, SLOTS])
        sm = sb("sm", [P, 3, 4 * HEADS])
        MN = sb("MN", [P, 4, SLOTS])
        WH = sb("WH", [P, HEADS, SLOTS])
        WQ = [sb(f"WQ{i}", [P, GT, KC, HEADS]) for i in range(2)]
        target = [sb(f"target{i}", [P, CH]) for i in range(2)]
        zrow = sb("zrow", [1, ROW])
        ptick = sb("ptick", [1, 2])
        tick = sb("tick", [P, 256])
        cells = itertools.count()

        def tick_cell():
            n = next(cells)
            return tick[:, n:n + 1]

        arena = sb("arena", [P, 7 * N + 384])

        def at(start, size):
            assert start + size <= 7 * N + 384
            return arena[:, start:start + size]

        A = [at(r * N, N) for r in range(4)]
        junk = at(4 * N, N // 4).bitcast(mybir.dt.int8)
        HG1 = [at(4 * N + N // 4 + i * KC * P, KC * P).rearrange("p (c f) -> p c f", f=P) for i in range(2)]
        at1 = 4 * N + N // 4 + 2 * KC * P
        D1 = [at(at1 + i * KC * 2 * P, KC * 2 * P).rearrange("p (c w i) -> p c w i", w=2, i=P) for i in range(GT)]
        HG2 = [at(i * CH * ROW, CH * ROW).rearrange("p (c f) -> p c f", f=ROW) for i in range(2)]
        at2 = 2 * CH * ROW
        at3 = at2 + 3 * KC * G3
        OH2 = [at(at3 + i * KC * P, KC * P).rearrange("p (c i) -> p c i", i=P) for i in range(2)]
        at4 = at3 + 2 * KC * P
        NS = at(at4, HEADS * GP).rearrange("p (h i) -> p h i", h=HEADS)
        SN = at(at4 + HEADS * GP, GP)
        SC1 = [NST[:, k * GP:(k + 1) * GP] for k in range(6)]
        SC2 = [at(at4 + (HEADS + 1 + k) * GP, GP) for k in range(6)]
        gA, gB, gC, gEp, gEm, gW = (at(k * N, N) for k in range(6))
        gH = at(6 * N, 2 * P)
        gN = at(6 * N + 2 * P, G3).rearrange("p (h i) -> p h i", h=HEADS)
        off = at(6 * N + 2 * P + G3, P)
        gmx = sb("gmx", [P, 4])
        gH2 = sb("gH2", [P, 2 * HEADS])

        xg = [sb(f"xg{i}", [P, GP]) for i in range(2)]
        at5 = at4 + (HEADS + 7) * GP
        D2 = [x.rearrange("p (c h i) -> p c h i", h=HEADS, i=P) for x in
              [at(at2 + i * KC * G3, KC * G3) for i in range(GT - 1)] + [NST[:, 0:KC * G3]]]
        gs = at(at5, GP)
        yc, yo = (at(at5 + k * GP, GP).rearrange("p (t f) -> p t f", f=P) for k in (1, 2))
        st6 = sb("st6", [P, GT, 6])
        mv = sb("mv", [P, GT, 2])
        rstd = sb("rstd", [P, GT])

        GR = pb("GR", [P, 4, GP])
        B = [pb(f"B{i}", [P, 4 * P]) for i in range(4)] + [GR[:, 0, :]]

        block = ctx.enter_context(nc.Block())
        setup_in = sem("setup_in")
        constants_made = sem("constants_made")
        gate_biases = sem("gate_biases")
        u_made, u_copied = sem("u_made"), sem("u_copied")
        a_in = [sem(f"a_in{r}") for r in range(4)]
        maxima_found = sem("maxima_found")
        tile_scanned = sem("tile_scanned")
        signs_half, signs_counted = sem("signs_half"), sem("signs_counted")
        select_step = sem("select_step")
        indices_made = sem("indices_made")
        ones_made = sem("ones_made")
        weighed, weighed_by_pool = sem("weighed"), sem("weighed_by_pool")
        h_in = [sem(f"h_in{r}") for r in range(2)]
        carry_step = sem("carry_step")
        sums_done, sums_read = sem("sums_done"), sem("sums_read")
        score_sums = sem("score_sums")
        scores_done = sem("scores_done")
        edge_step = sem("edge_step")
        check_step, check_total = sem("check_step"), sem("check_total")
        flag_set = sem("flag_set")
        zeros_made = sem("zeros_made")
        table_in = sem("table_in")
        x_in = [sem(f"x_in{i}") for i in range(2)]
        indices_copied = sem("indices_copied")
        h2_in = [sem(f"h2_in{r}") for r in range(2)]
        softmax_step = sem("softmax_step")
        exp_turn = sem("exp_turn")
        ones2_made = sem("ones2_made")
        spread_by_dve, spread_by_act = sem("spread_by_dve"), sem("spread_by_act")
        heads_done, heads_read = sem("heads_done"), sem("heads_read")
        w_product, mean_copied = sem("w_product"), sem("mean_copied")
        fe, fn, gf = ({k: sem(pre + k) for k in ("gates", "tanh", "pre", "n", "new", "chain")} for pre in ("fe_", "fn_", "gf_"))
        y, gy = ({k: sem(pre + k) for k in ("sum", "tr", "y", "sq", "norm", "out", "chain")} for pre in ("y_", "gy_"))
        gx_in = sem("gx_in")
        g = {k: sem("g_" + k) for k in (
            "ld", "at", "off", "off2", "pm", "mm", "ev", "e", "ed", "eg", "a", "aoff", "ep", "att", "mx",
            "ex", "w", "tr", "cp", "num", "nev", "sup", "sev", "chain")}
        LOADS = 16 * 14

        def arrived_x(eng, n, par):
            eng.wait_ge(x_in[par], (n - par) * 8 + 16)

        def arrived(eng, G, par):
            eng.wait_ge(h2_in[par], (G - par) * (8 * CH) + 16 * CH)

        def gates(pe, s, n, k, src, x):
            pe.wait_ge(s["pre"], n + 1)
            for b in range(2):
                nc.tensor.matmul(GR[:, b, :], Wi[:, k, b * P:(b + 1) * P], src, start=True, stop=False)
                nc.tensor.matmul(GR[:, b, :], Wh[:, k, b * P:(b + 1) * P], x, start=False, stop=True)
            nc.tensor.matmul(GR[:, 2, :], Wi[:, k, 2 * P:], src, start=True, stop=True)
            nc.tensor.matmul(GR[:, 3, :], Wh[:, k, 2 * P:], x, start=True, stop=True).then_inc(s["gates"], 1)

        def gates_act(act, s, n, k, sc, for_pool=False):
            act.wait_ge(s["gates"], n + 1)
            act.wait_ge(s["new"], n + 2)
            nc.scalar.activation(sc[0], GR[:, 0, :], ACT.Tanh, scale=0.5, bias=gb[:, k, 0:1])
            last = nc.scalar.activation(sc[1], GR[:, 1, :], ACT.Tanh, scale=0.5, bias=gb[:, k, 1:2])
            if for_pool:
                last.then_inc(s["chain"], 1)
                act.wait_ge(s["chain"], n + 1)
                nc.scalar.activation(sc[1], sc[1], ACT.Identity, scale=0.5, bias=half[:, 0:1])
                nc.scalar.activation(sc[3], GR[:, 2, :], ACT.Identity, bias=gb[:, k, 2:3])
            nc.scalar.activation(sc[2], GR[:, 3, :], ACT.Identity, scale=0.5, bias=gb[:, k, 3:4]).then_inc(s["tanh"], 1)

        def cand_act(act, s, n, k, sc, for_pool=False):
            act.wait_ge(s["pre"], n + 2)
            if for_pool:
                nc.scalar.activation(sc[5], sc[4], ACT.Tanh).then_inc(s["n"], 1)
            else:
                nc.scalar.activation(sc[5], sc[4], ACT.Tanh, bias=gb[:, k, 2:3]).then_inc(s["n"], 1)

        def cand_dve(dve, s, n, sc):
            dve.wait_ge(s["tanh"], n + 1)
            nc.vector.scalar_tensor_tensor(sc[4], sc[0], 1.0, sc[2], ALU.add, ALU.mult).then_inc(s["chain"], 1)
            dve.wait_ge(s["chain"], 3 * n + 1)
            nc.vector.tensor_tensor(sc[4], sc[4], GR[:, 2, :], ALU.add).then_inc(s["pre"], 1)

        def new_dve(dve, s, n, sc, x, dest):
            dve.wait_ge(s["n"], n + 1)
            nc.vector.tensor_tensor(sc[4], x, sc[5], ALU.subtract).then_inc(s["chain"], 1)
            dve.wait_ge(s["chain"], 3 * n + 2)
            nc.vector.scalar_tensor_tensor(sc[4], sc[1], 1.0, sc[4], ALU.add, ALU.mult).then_inc(s["chain"], 1)
            dve.wait_ge(s["chain"], 3 * n + 3)
            nc.vector.scalar_tensor_tensor(dest, sc[4], 0.5, sc[5], ALU.mult, ALU.add).then_inc(s["new"], 1)

        def sum_dve(dve, s, n, G, node, made):
            dve.wait_ge(*made)
            nc.vector.tensor_tensor(gs, node, ST[:, bass.ds(G * GP, GP)], ALU.add).then_inc(s["sum"], 1)

        def back_pe(pe, s, n):
            pe.wait_ge(s["sum"], n + 1)
            pe.wait_ge(s["y"], n + 1)
            for r in range(GT):
                last = nc.tensor.transpose(B[3][:, r * P:(r + 1) * P], gs[:, r * P:(r + 1) * P], ident[:, :])
            last.then_inc(s["tr"], 1)

        def y_dve(dve, s, n, G):
            dve.wait_ge(s["tr"], n + 1)
            dve.wait_ge(s["norm"], n + 1)
            for r in range(GT):
                last = nc.vector.scalar_tensor_tensor(yc[:, r, :], B[3][:, r * P:(r + 1) * P], diag[:, bass.ds(G * GT + r, 1)],
                                                      TX[:, bass.ds(G * GT + r, 1), 0:P].rearrange("p a f -> p (a f)"), ALU.mult, ALU.add)
            last.then_inc(s["chain"], 1)
            dve.wait_ge(s["chain"], 3 * n + 1)
            nc.vector.memset(tick_cell(), 0.0)
            for r in range(GT):
                last = nc.vector.bn_stats(st6[:, r, :], yc[:, r, :])
            last.then_inc(s["chain"], 1)
            dve.wait_ge(s["chain"], 3 * n + 2)
            nc.vector.memset(tick_cell(), 0.0)
            for r in range(GT):
                last = nc.vector.bn_aggr(mv[:, r, :], st6[:, r, :])
            last.then_inc(s["y"], 1)

        def dev_act(act, s, n):
            act.wait_ge(s["y"], n + 2)
            nc.scalar.activation(rstd[:, :], mv[:, :, 1], ACT.Sqrt, bias=eps[:, 0:1]).then_inc(s["sq"], 1)

        def norm_dve(dve, s, n):
            dve.wait_ge(s["sq"], n + 1)
            nc.vector.reciprocal(rstd[:, :], rstd[:, :]).then_inc(s["chain"], 1)
            dve.wait_ge(s["chain"], 3 * n + 3)
            dve.wait_ge(s["out"], 16 * (n + 1))
            for r in range(GT):
                last = nc.vector.tensor_scalar(yo[:, r, :], yc[:, r, :], mv[:, r, 0:1], rstd[:, r:r + 1], ALU.subtract, ALU.mult)
            last.then_inc(s["norm"], 1)

        def store(sp, s, n):
            sp.wait_ge(s["norm"], n + 2)
            sp.dma_start(out.rearrange("(t p) f -> p t f", p=P)[:, bass.ds(n * GT, GT), :], yo).then_inc(s["out"], 16)

        def rest(eng, run):
            eng.wait_ge(flag_set, 1)
            with eng.If(eng.value_load(flag[0:1, 0:1], min_val=0, max_val=1) > 0):
                run()

        @block.sync
        def _(sp):
            def load_adj(G):
                for r in range(GT):
                    t = G * GT + r
                    sp.wait_ge(tile_scanned, t + 1)
                    sp.wait_ge(signs_counted, t + 1)
                    sp.dma_start(A[r], d["adj"][bass.ds(t * P, P), :]).then_inc(a_in[r], 16)

            def load_x(G, par, done):
                sp.wait_ge(done, G + 1)
                sp.dma_start(xg[par][:, :], d["xT"][:, bass.ds(G * GP, GP)]).then_inc(x_in[par], 16)

            load_adj(0)
            with nc.allow_non_contiguous_dma(reason="small"):
                sp.dma_start(TX[:, :, 0:P], d["x1"][1:N + 1, :].rearrange("(t p) f -> p t f", p=P)).then_inc(setup_in, 16)
                sp.dma_start(iota[:, :], d["iota"]).then_inc(setup_in, 16)
                sp.dma_start(W[:, :, :], d["gatW"]).then_inc(setup_in, 16)
                sp.dma_start(WT[:, :, :], d["gatWT"]).then_inc(setup_in, 16)
                sp.dma_start(a12[:, :], d["a12"]).then_inc(setup_in, 16)
                sp.dma_start(diag[:, :], d["diag"]).then_inc(setup_in, 16)
                sp.dma_start(Wi[:, :, :], d["Wi"]).then_inc(setup_in, 16)
                sp.dma_start(Wh[:, :, :], d["Wh"]).then_inc(setup_in, 16)
                sp.dma_start(bT[:, :, :], d["b"]).then_inc(setup_in, 16)
                sp.dma_start(ident[:, :], d["ident"]).then_inc(setup_in, 16)
                sp.dma_start(rq[:, :], d["rq"]).then_inc(setup_in, 16)
                sp.dma_start(bounds[:, :, :], d["bounds"]).then_inc(setup_in, 16)
                sp.dma_start(seg1[:, :], d["seg1"]).then_inc(setup_in, 16)
                sp.dma_start(dkey[:, :], d["dkey"]).then_inc(setup_in, 16)
            with sp.Fori(0, NG // 2 - 1) as it:
                for u in range(2):
                    load_adj(it * 2 + 1 + u)
                    load_x(it * 2 + u, u, fe["new"])
            load_adj(NG - 1)
            load_x(NG - 2, 0, fe["new"])
            sp.wait_ge(zeros_made, 1)
            sp.dma_start(table[0:1, :], zrow[0:1, :]).then_inc(table_in, 16)
            for k in range(4):
                part = (slice(0, 10), slice(10, 20), slice(20, T - GT), slice(T - GT, T))[k]
                sp.wait_ge(scores_done, 1 if k < 3 else 2)
                sp.dma_start(table[1 + part.start * P:1 + part.stop * P, :].rearrange("(t p) f -> p t f", p=P), TX[:, part, :]).then_inc(table_in, 16)
            load_x(NG - 1, 1, fe["new"])
            sp.wait_ge(fe["new"], NG + 2)
            load_x(0, 0, fn["new"])
            load_x(1, 1, fn["new"])
            with sp.Fori(1, NG // 2) as it:
                for u in range(2):
                    load_x(it * 2 + u, u, fn["new"])
                    store(sp, y, it * 2 + u - 2)
            store(sp, y, NG - 2)
            store(sp, y, NG - 1)
            sp.wait_ge(y["out"], 16 * (NG + 1))

            def general():
                sp.dma_start(off, d["off"]).then_inc(g["ld"], 16)
                adjT = d["adjT"].rearrange("(j p) i -> p j i", p=P)
                with sp.Fori(0, T) as t:
                    sp.wait_ge(g["mm"], t + 1)
                    sp.dma_start(gA[:, :].rearrange("p (j i) -> p j i", i=P), adjT[:, :, bass.ds(t * P, P)]).then_inc(g["at"], 16)
                sp.wait_ge(g["ed"], T + 1)
                with nc.allow_non_contiguous_dma(reason="the scores as rows"):
                    for k in range(2 * HEADS):
                        sp.dma_start(e_dram[k, :].rearrange("(t p) -> p t", p=P), E6[:, :, k]).then_inc(g["eg"], 16)
                sp.wait_ge(g["eg"], 16 * 2 * HEADS)
                with sp.Fori(0, T) as t:
                    sp.wait_ge(g["w"], t * HEADS + 1)
                    sp.dma_start(gA[:, :], d["adj"][bass.ds(t * P, P), :]).then_inc(g["a"], 16)
                    for h in range(HEADS):
                        sp.wait_ge(g["att"], t * HEADS + h + 1)
                        sp.dma_start(gEp[:, :], e_dram[h:h + 1, :].to_broadcast([P, N])).then_inc(g["ep"], 16)
                        sp.dma_start(gEm[:, :], e_dram[HEADS + h:HEADS + h + 1, :].to_broadcast([P, N])).then_inc(g["ep"], 16)
                with sp.Fori(0, NG) as G:
                    sp.wait_ge(gf["new"], G * 2 + 2)
                    sp.dma_start(xg[0][:, :], d["xT"][:, bass.ds(G * GP, GP)]).then_inc(gx_in, 16)
                    store(sp, gy, G)
                sp.wait_ge(gy["out"], 16 * (NG + 1))

            rest(sp, general)

        @block.gpsimd
        def _(pool):
            nc.gpsimd.memset(ones[:, :], 1.0).then_inc(constants_made, 1)
            nc.gpsimd.memset(eps[:, :], EPS).then_inc(constants_made, 1)
            nc.gpsimd.memset(half[:, :], 0.5).then_inc(constants_made, 1)
            pool.sem_inc(fe["pre"], 1)
            pool.sem_inc(fe["new"], 2)
            nc.gpsimd.memset(TX[:, :, P:], 0.0).then_inc(constants_made, 1)
            nc.gpsimd.memset(ptick[:, :], 0.0).then_inc(carry_step, 1)
            nc.gpsimd.memset(zrow[:, :], 0.0).then_inc(zeros_made, 1)
            pool.wait_ge(zeros_made, 1)
            last_row = pool.to_reg(N)
            pool.wait_ge(setup_in, LOADS)
            for k in range(2):
                nc.gpsimd.tensor_tensor(gb[:, k, 0:2], bT[:, 2 * k, 0:2], bT[:, 2 * k + 1, 0:2], ALU.add).then_inc(gate_biases, 1)
                nc.gpsimd.tensor_copy(gb[:, k, 2:3], bT[:, 2 * k, 2:3]).then_inc(gate_biases, 1)
                nc.gpsimd.tensor_scalar(gb[:, k, 3:4], bT[:, 2 * k + 1, 2:3], 0.5, None, ALU.mult).then_inc(gate_biases, 1)
            pool.wait_ge(gate_biases, 6)
            nc.gpsimd.tensor_scalar(gb[:, :, 0:2], gb[:, :, 0:2], 0.5, None, ALU.mult).then_inc(gate_biases, 1)

            def carry(n):
                pool.wait_ge(carry_step, n + 1)
                nc.gpsimd.tensor_tensor(ptick[0:1, 1:2], ptick[0:1, 0:1], ptick[0:1, 0:1], ALU.add).then_inc(carry_step, 1)

            def tt(o, a, b, op, s):
                return nc.gpsimd.tensor_tensor(o, a, b, op).then_inc(s, 1)

            def cand_pool(n):
                pool.wait_ge(fe["tanh"], n + 1)
                tt(SC1[4], SC1[0], SC1[2], ALU.mult, edge_step)
                pool.wait_ge(edge_step, n * 4 + 1)
                tt(SC1[4], SC1[4], SC1[2], ALU.add, edge_step)
                pool.wait_ge(edge_step, n * 4 + 2)
                tt(SC1[4], SC1[4], SC1[3], ALU.add, fe["pre"])

            def new_pool(n, par):
                pool.wait_ge(fe["n"], n + 1)
                tt(SC1[4], xg[par][:, :], SC1[5], ALU.subtract, edge_step)
                pool.wait_ge(edge_step, n * 4 + 3)
                tt(SC1[4], SC1[4], SC1[1], ALU.mult, edge_step)
                pool.wait_ge(edge_step, n * 4 + 4)
                tt(ST[:, bass.ds(n * GP, GP)], SC1[4], SC1[5], ALU.add, fe["new"])

            def weigh_pool(G, par):
                r = GT - 1
                pool.wait_ge(ones_made, G * GT + r + 1)
                nc.gpsimd.tensor_tensor(D1[r][:, :, 0, :], D1[r][:, :, 1, :], vQ[par][:, r * KC:(r + 1) * KC].unsqueeze(2).to_broadcast([P, KC, P]),
                                        ALU.mult).then_inc(weighed_by_pool, 1)

            def gather1(G, par, edge):
                pool.wait_ge(indices_made, G + 1)
                for r in range(GT):
                    pool.wait_ge(sums_done, G * GT + r + 7)
                    carry(G * GT + r)
                    for c in range(KC):
                        n = r * KC + c
                        pool.indirect_dma_start(HG1[r % 2][:, c, :], None, d["x1"], bass.IndirectOffsetOnAxis(idx[par][:, n:n + 1], axis=0),
                                                bounds_check=last_row, oob_is_err=False).then_inc(h_in[r % 2], 16)
                    if r == 0:
                        weigh_pool(G, par)
                    if edge and r == 1:
                        cand_pool(G - 1)
                    if edge and r == 2:
                        new_pool(G - 1, 1 - par)

            gather1(0, 0, False)
            with pool.Fori(0, NG // 2 - 2) as it:
                gather1(it * 2 + 1, 1, True)
                gather1(it * 2 + 2, 0, True)
            gather1(NG - 3, 1, True)
            gather1(NG - 2, 0, False)
            gather1(NG - 1, 1, False)
            def indices(G, par):
                nc.gpsimd.tensor_copy(idx[par][:, :], IDX[:, bass.ds(G, 1), :].rearrange("p a c -> p (a c)")).then_inc(indices_copied, 1)

            def gather2(G, par, ahead):
                pool.wait_ge(indices_copied, G + 1)
                for r in range(GT):
                    pool.wait_ge(heads_done, G * GT + r + 1)
                    if ahead and r == GT - 1:
                        if ahead != "first":
                            arrived(pool, G - 1, 1 - par)
                        carry(T + G * GT + r)
                        indices(G + 1, 1 - par)
                    else:
                        carry(T + G * GT + r)
                    for n in range(r * KC, (r + 1) * KC):
                        pool.indirect_dma_start(HG2[par][:, n, :], None, table, bass.IndirectOffsetOnAxis(idx[par][:, n:n + 1], axis=0),
                                                bounds_check=last_row, oob_is_err=False).then_inc(h2_in[par], 16)

            pool.wait_ge(sums_done, T + 8)
            indices(0, 0)
            pool.wait_ge(table_in, 16 * 5)
            gather2(0, 0, "first")
            with pool.Fori(0, NG // 2 - 1) as it:
                gather2(it * 2 + 1, 1, True)
                gather2(it * 2 + 2, 0, True)
            gather2(NG - 1, 1, False)

        @block.vector
        def _(dve):
            dve.sem_inc(g["w"], 1)
            dve.sem_inc(g["att"], 1)
            for s in (y, gy):
                dve.sem_inc(s["y"], 1)
                dve.sem_inc(s["norm"], 1)
            for s in (fn, gf):
                dve.sem_inc(s["pre"], 1)
            dve.sem_inc(fn["new"], 2)
            dve.sem_inc(gf["new"], 2)
            dve.sem_inc(y["out"], 16)
            dve.sem_inc(gy["out"], 16)
            dve.sem_inc(tile_scanned, 4)
            dve.sem_inc(g["ed"], 1)
            def chain(sem, base):
                count = [0]

                def done(ins, wait=True):
                    ins.then_inc(sem, 1)
                    count[0] += 1
                    if wait:
                        dve.wait_ge(sem, base + count[0])
                return done, count

            def carry():
                nc.vector.memset(tick_cell(), 0.0)

            SEL = 65
            AHEAD = 8

            SCAN = 8 * GT

            def scan(G, n):
                r, s = n // 8, n % 4
                row = A[r][:, s * SEG:(s + 1) * SEG]
                if n % 8 == 0:
                    dve.wait_ge(a_in[r], 16 * (G + 1))
                    carry()
                if n % 8 < 4:
                    last = nc.vector.max(V[:, r, 8 * s:8 * s + 8], row)
                    if s == 3:
                        last.then_inc(maxima_found, 1)
                    return
                if s == 0:
                    dve.wait_ge(maxima_found, G * GT + r + 1)
                    carry()
                last = nc.vector.max_index(I[:, r, 8 * s:8 * s + 8], V[:, r, 8 * s:8 * s + 8], row)
                if s == 3:
                    last.then_inc(tile_scanned, 1)

            def select(G, par, ahead):
                own, count = chain(select_step, G * SEL)
                scanned = [0]

                def done(ins, wait=True):
                    own(ins, False)
                    if ahead and wait and count[0] > 7 and scanned[0] < AHEAD:
                        scan(G + 1, scanned[0])
                        scanned[0] += 1
                    if wait:
                        dve.wait_ge(select_step, G * SEL + count[0])

                flat = lambda x: x.rearrange("p a b -> p (a b)")
                Vf, Vu = flat(V[:, :, :]), flat(V[:, :, :]).bitcast(u32)
                done(nc.vector.tensor_tensor(K0[:, :], flat(I[:, :, :]), seg1[:, :], ALU.add))
                done(nc.vector.scalar_tensor_tensor(K0[:, :], Vf, 0.0, K0[:, :], ALU.is_gt, ALU.mult))
                done(nc.vector.tensor_tensor(K[:, :].rearrange("p (r c) -> p r c", c=CAND), K0[:, :].rearrange("p (r c) -> p r c", c=CAND),
                                             dkey[:, bass.ds(G * GT, GT)].unsqueeze(2).to_broadcast([P, GT, CAND]), ALU.not_equal))
                done(nc.vector.tensor_tensor(K[:, :], K[:, :], K0[:, :], ALU.mult))
                done(nc.vector.tensor_scalar(Ks[:, :], K[:, :], float(KEY0), 65536.0, ALU.add, ALU.mult))
                done(nc.vector.scalar_tensor_tensor(KK[:, 0, :], Vu, 16, Ks[:, :], ALU.logical_shift_right, ALU.bitwise_or), False)
                done(nc.vector.scalar_tensor_tensor(KK[:, 1, :], Vu, 65535, Ks[:, :], ALU.bitwise_and, ALU.bitwise_or))
                KF = KK[:, :, :].bitcast(fp32)
                for t in range(GT):
                    for b in range(4):
                        done(nc.vector.tensor_copy(QK[Q * t:Q * (t + 1), 0, :, b, :], KF[Q * b:Q * (b + 1), :, t * CAND:(t + 1) * CAND]), t == 3 and b == 3)
                for m in range(RND):
                    old, new = (QK[:, n % 2, :, :, :].rearrange("p w b c -> p w (b c)") for n in (m, m + 1))
                    carry()
                    for w in range(2):
                        last = nc.vector.max(S[:, w, 8 * m:8 * m + 8], old[:, w, :])
                    done(last)
                    if m + 1 < RND:
                        carry()
                        for w in range(2):
                            last = nc.vector.match_replace(new[:, w, :], S[:, w, 8 * m:8 * m + 8], old[:, w, :], 0.0)
                        done(last)
                S1, S2 = (S[:, w, 0:SLOTS].bitcast(u32) for w in range(2))
                done(nc.vector.tensor_scalar(Ku[:, 0, :], S1, 16, None, ALU.logical_shift_right), False)
                done(nc.vector.tensor_scalar(Ku[:, 1, :], S2, 65535, None, ALU.bitwise_and))
                done(nc.vector.scalar_tensor_tensor(Ku[:, 1, :], S1, 16, Ku[:, 1, :], ALU.logical_shift_left, ALU.bitwise_or), False)
                done(nc.vector.tensor_scalar(F[:, 3, :], Ku[:, 0, :], float(KEY0), None, ALU.subtract))
                done(nc.vector.scalar_tensor_tensor(F[:, 1, :], F[:, 3, :], 0.0, Ku[:, 1, :].bitcast(fp32), ALU.is_gt, ALU.mult), False)
                key4 = F[:, 3, :].unsqueeze(1).to_broadcast([P, 4, SLOTS])
                limit = lambda w: bounds[:, w, :].unsqueeze(2).to_broadcast([P, 4, SLOTS])
                mb = MB[:, bass.ds(G, 1), :, :].rearrange("p a b s -> p (a b) s")
                done(nc.vector.tensor_scalar(F[:, 2, :], F[:, 3, :], float(N), None, ALU.is_gt), False)
                done(nc.vector.tensor_tensor(MH[:, :, :], key4, limit(0), ALU.is_gt), False)
                done(nc.vector.tensor_tensor(MN[:, :, :], key4, limit(1), ALU.is_le))
                done(nc.vector.tensor_tensor(mb, MH[:, :, :], MN[:, :, :], ALU.mult), False)
                done(nc.vector.scalar_tensor_tensor(F[:, 2, :], F[:, 3, :], 2.0 * N, F[:, 2, :], ALU.is_gt, ALU.add))
                done(nc.vector.scalar_tensor_tensor(F[:, 2, :], F[:, 3, :], 3.0 * N, F[:, 2, :], ALU.is_gt, ALU.add))
                done(nc.vector.scalar_tensor_tensor(F[:, 0, :], F[:, 2, :], -float(N), F[:, 3, :], ALU.mult, ALU.add))
                done(nc.vector.tensor_copy(AV[:, bass.ds(G, 1), :].rearrange("p a s -> p (a s)"), F[:, 1, :]), False)
                for q in range(4):
                    for t in range(GT):
                        done(nc.vector.tensor_copy(QF[Q * q:Q * (q + 1), :, t, :],
                                                   F[Q * t:Q * (t + 1), 0:3, :].rearrange("p w (k q) -> p w k q", q=4)[:, :, :, q]), q == 3 and t == GT - 1)
                dve.wait_ge(sums_done, G * GT + 4)
                keys, vals, rows = (QF[:, w, :, :].rearrange("p t k -> p (t k)") for w in range(3))
                carry()
                nc.vector.tensor_copy(idx[par][:, :], keys).then_inc(indices_made, 1)
                done(nc.vector.tensor_copy(vQ[par][:, :], vals), False)
                done(nc.vector.tensor_copy(IDX[:, bass.ds(G, 1), :].rearrange("p a c -> p (a c)"), keys), False)
                done(nc.vector.tensor_scalar(target[par][:, :], rows, float(Q), rq[:, 0:1], ALU.mult, ALU.add))
                done(nc.vector.tensor_copy(TG[:, bass.ds(G, 1), :].rearrange("p a c -> p (a c)"), target[par][:, :]), False)
                for r in range(GT):
                    dve.wait_ge(sums_done, G * GT + r + 5)
                    last = nc.vector.tensor_tensor(D1[r][:, :, 1, :], iota[:, :].unsqueeze(1).to_broadcast([P, KC, P]),
                                                   target[par][:, r * KC:(r + 1) * KC].unsqueeze(2).to_broadcast([P, KC, P]), ALU.is_equal)
                    last.then_inc(ones_made, 1)
                assert count[0] == SEL, count[0]
                if ahead:
                    for n in range(scanned[0], SCAN):
                        scan(G + 1, n)
                    dve.wait_ge(tile_scanned, (G + 2) * GT + 4)

            for n in range(SCAN):
                scan(0, n)
            dve.wait_ge(tile_scanned, GT + 4)
            dve.wait_ge(setup_in, LOADS)
            with dve.Fori(0, NG // 2 - 1) as it:
                select(it * 2, 0, True)
                select(it * 2 + 1, 1, True)
            select(NG - 2, 0, False)
            for n in range(SCAN):
                scan(NG - 1, n)
            dve.wait_ge(tile_scanned, T + 4)
            select(NG - 1, 1, False)
            dve.wait_ge(signs_counted, T + 4)
            done, count = chain(check_step, 0)
            done(nc.vector.tensor_reduce(chk[:, 0:1], MB[:, :, :, :].rearrange("p a b s -> p (a b s)"), AX.X, ALU.add), False)
            done(nc.vector.tensor_scalar(E6[:, :, 0], diag[:, :], 0.0, None, ALU.is_gt))
            done(nc.vector.tensor_tensor(E6[:, :, 1], sgn[:, :, 0], E6[:, :, 0], ALU.subtract))
            done(nc.vector.tensor_reduce(chk[:, 1:2], E6[:, :, 1], AX.X, ALU.add), False)
            done(nc.vector.tensor_reduce(chk[:, 3:4], sgn[:, :, 1], AX.X, ALU.add))
            nc.vector.tensor_tensor(chk[:, 2:3], chk[:, 1:2], chk[:, 0:1], ALU.subtract).then_inc(check_total, 1)
            for a, b, bank in ((0, T - GT, B[2]), (T - GT, T, B[3])):
                EB = bank[:, 0:T * HEADS].rearrange("p (t h) -> p t h", h=HEADS)
                dve.wait_ge(score_sums, b)
                done(nc.vector.tensor_scalar(E6[:, a:b, 0:HEADS], EB[:, a:b, :], ALPHA, None, ALU.mult))
                nc.vector.tensor_tensor(TX[:, a:b, P:P + HEADS], E6[:, a:b, 0:HEADS], EB[:, a:b, :], ALU.max).then_inc(scores_done, 1)
            dve.wait_ge(scores_done, 2)
            dve.wait_ge(check_total, 2)
            done(nc.vector.tensor_scalar(chk[0:1, 4:5], B[3][0:1, P:P + 1], 0.0, None, ALU.not_equal))
            nc.vector.scalar_tensor_tensor(flag[0:1, 0:1], B[3][0:1, P + 1:P + 2], 0.0, chk[0:1, 4:5], ALU.not_equal, ALU.max).then_inc(flag_set, 1)
            for n in range(NG - 3, NG):
                dve.wait_ge(fe["tanh"], n + 1)
                done(nc.vector.scalar_tensor_tensor(SC1[4], SC1[0], 1.0, SC1[2], ALU.add, ALU.mult))
                nc.vector.tensor_tensor(SC1[4], SC1[4], SC1[3], ALU.add).then_inc(fe["pre"], 1)
                dve.wait_ge(fe["n"], n + 1)
                done(nc.vector.tensor_tensor(SC1[4], xg[n % 2][:, :], SC1[5], ALU.subtract))
                done(nc.vector.tensor_tensor(SC1[4], SC1[4], SC1[1], ALU.mult))
                nc.vector.tensor_tensor(ST[:, n * GP:(n + 1) * GP], SC1[4], SC1[5], ALU.add).then_inc(fe["new"], 1)

            SOFT, SOFTA = 43, 21

            def scores(G, par):
                done, count = chain(softmax_step, G * SOFT)
                arrived(dve, G, par)
                H = HG2[par].rearrange("p (t k) f -> p t k f", k=KC)
                B4 = lambda x: x[:, :, :].rearrange("p (b h) s -> p b h s", h=HEADS)
                for q in range(4):
                    for t in range(GT):
                        o = EQ[Q * t:Q * (t + 1), :, :].rearrange("p h (k q) -> p k h q", q=4)[:, :, :, q]
                        done(nc.vector.tensor_copy(o, H[Q * q:Q * (q + 1), t, :, P:P + HEADS]), q == 3 and t == GT - 1)
                mb = MB[:, bass.ds(G, 1), :, :].rearrange("p a b s -> p (a b) s")
                each_head = lambda x: x.unsqueeze(2).to_broadcast([P, 4, HEADS, SLOTS])
                each_row = lambda x: x.unsqueeze(1).to_broadcast([P, 4, HEADS, SLOTS])
                done(nc.vector.tensor_scalar(MN[:, :, :], mb, 1.0, -NEG_INF, ALU.subtract, ALU.mult), False)
                done(nc.vector.tensor_tensor(B4(ER), each_row(EQ[:, :, :]), each_head(mb), ALU.mult))
                done(nc.vector.tensor_tensor(B4(ER), B4(ER), each_head(MN[:, :, :]), ALU.add))
                done(nc.vector.tensor_reduce(sm[:, 0, :], ER[:, :, :], AX.X, ALU.max))
                nc.vector.tensor_tensor(ER[:, :, :], ER[:, :, :], sm[:, 0, :].unsqueeze(2).to_broadcast([P, 4 * HEADS, SLOTS]), ALU.subtract).then_inc(exp_turn, 1)
                done(nc.vector.tensor_copy(target[par][:, :], TG[:, bass.ds(G, 1), :].rearrange("p a c -> p (a c)")), False)
                assert count[0] == SOFTA, count[0]

            def softmax(G, par):
                done, count = chain(softmax_step, G * SOFT + SOFTA)
                B4 = lambda x: x[:, :, :].rearrange("p (b h) s -> p b h s", h=HEADS)
                mb = MB[:, bass.ds(G, 1), :, :].rearrange("p a b s -> p (a b) s")
                each_head = lambda x: x.unsqueeze(2).to_broadcast([P, 4, HEADS, SLOTS])
                dve.wait_ge(exp_turn, 2 * G + 2)
                done(nc.vector.tensor_reduce(sm[:, 1, :], ER[:, :, :], AX.X, ALU.add))
                done(nc.vector.tensor_tensor(B4(ER), B4(ER), each_head(mb), ALU.mult), False)
                done(nc.vector.reciprocal(sm[:, 2, :], sm[:, 1, :]))
                done(nc.vector.tensor_tensor(ER[:, :, :], ER[:, :, :], sm[:, 2, :].unsqueeze(2).to_broadcast([P, 4 * HEADS, SLOTS]), ALU.mult))
                done(nc.vector.tensor_reduce(WH[:, :, :], B4(ER).rearrange("p b h s -> p h s b"), AX.X, ALU.add))
                av = AV[:, bass.ds(G, 1), :].to_broadcast([P, HEADS, SLOTS])
                done(nc.vector.tensor_tensor(WH[:, :, :], WH[:, :, :], av, ALU.mult))
                for q in range(4):
                    for t in range(GT):
                        i_ = WH[Q * t:Q * (t + 1), :, :].rearrange("p h (k q) -> p k h q", q=4)[:, :, :, q]
                        done(nc.vector.tensor_copy(WQ[par][Q * q:Q * (q + 1), t, :, :], i_), q == 3 and t == GT - 1)
                assert count[0] + SOFTA == SOFT, count[0]

            def spread(t, r, par, heads):
                dve.wait_ge(heads_done, t + 5)
                dve.wait_ge(spread_by_act, t + 1)
                of = target[par][:, r * KC:(r + 1) * KC].unsqueeze(2).to_broadcast([P, KC, P])
                nc.vector.tensor_tensor(OH2[r % 2], iota[:, :].unsqueeze(1).to_broadcast([P, KC, P]), of, ALU.is_equal).then_inc(ones2_made, 1)
                dve.wait_ge(ones2_made, t + 1)
                for h in range(heads):
                    last = nc.vector.tensor_tensor(D2[r][:, :, h, :], OH2[r % 2], WQ[par][:, r, :, h:h + 1].to_broadcast([P, KC, P]), ALU.mult)
                last.then_inc(spread_by_dve, 1)

            def node_sum(m, par):
                new_dve(dve, fn, m, SC2, xg[par][:, :], gs)
                sum_dve(dve, y, m, m, gs, (fn["new"], m + 3))

            def step(G, par, node, ahead):
                heads = 1 if ahead else 2
                if node and not ahead:
                    cand_dve(dve, fn, G - 2, SC2)
                spread(G * GT, 0, par, heads)
                if node and ahead:
                    cand_dve(dve, fn, G - 2, SC2)
                spread(G * GT + 1, 1, par, heads)
                if node:
                    node_sum(G - 2, par)
                spread(G * GT + 2, 2, par, heads)
                if ahead:
                    scores(G + 1, 1 - par)
                spread(G * GT + 3, 3, par, heads)
                if node:
                    y_dve(dve, y, G - 2, G - 2)
                if ahead:
                    softmax(G + 1, 1 - par)
                if node:
                    norm_dve(dve, y, G - 2)

            dve.wait_ge(fe["new"], NG + 2)
            scores(0, 0)
            softmax(0, 0)
            step(0, 0, False, True)
            step(1, 1, False, True)
            with dve.Fori(1, NG // 2 - 1) as it:
                step(it * 2, 0, True, True)
                step(it * 2 + 1, 1, True, True)
            step(NG - 2, 0, True, True)
            step(NG - 1, 1, True, False)
            for par in range(2):
                m = NG - 2 + par
                cand_dve(dve, fn, m, SC2)
                node_sum(m, par)
                y_dve(dve, y, m, m)
                norm_dve(dve, y, m)

            def general():
                dve.wait_ge(y["out"], 16 * (NG + 1))
                dve.wait_ge(g["ld"], 16)
                with dve.Fori(0, T) as t:
                    dve.wait_ge(g["at"], 16 * (t + 1))
                    blk = gA[:, bass.ds(t * P, P)]
                    nc.vector.tensor_tensor(blk, blk, off, ALU.mult).then_inc(g["off"], 1)
                    dve.wait_ge(g["off"], t + 1)
                    nc.vector.tensor_scalar(gB[:, :], gA[:, :], 0.0, None, ALU.is_gt)
                    nc.vector.tensor_scalar(gC[:, :], gA[:, :], 0.0, None, ALU.is_lt).then_inc(g["pm"], 1)
                    dve.wait_ge(g["e"], t + 1)
                    nc.vector.tensor_scalar(gH2[:, :], B[4][:, 0:6], ALPHA, None, ALU.mult).then_inc(g["off2"], 1)
                    dve.wait_ge(g["off2"], t + 1)
                    nc.vector.tensor_tensor(E6[:, bass.ds(t, 1), :].rearrange("p a f -> p (a f)"), B[4][:, 0:6], gH2[:, :], ALU.max).then_inc(g["ed"], 1)
                with dve.Fori(0, T) as t:
                    dve.wait_ge(g["a"], 16 * (t + 1))
                    blk = gA[:, bass.ds(t * P, P)]
                    nc.vector.tensor_tensor(blk, blk, off, ALU.mult).then_inc(g["aoff"], 1)
                    dve.wait_ge(g["aoff"], t + 1)
                    for h in range(HEADS):
                        i = t * HEADS + h
                        c = [0]

                        def link(ins):
                            ins.then_inc(g["chain"], 1)
                            c[0] += 1
                            dve.wait_ge(g["chain"], i * 5 + c[0])

                        dve.wait_ge(g["ep"], 32 * (i + 1))
                        dve.wait_ge(g["tr"], 8 * i + 1)
                        link(nc.vector.scalar_tensor_tensor(gB[:, :], gA[:, :], 0.0, gEp[:, :], ALU.is_gt, ALU.mult))
                        link(nc.vector.scalar_tensor_tensor(gC[:, :], gA[:, :], 0.0, gEm[:, :], ALU.is_lt, ALU.mult))
                        nc.vector.tensor_tensor(gB[:, :], gB[:, :], gC[:, :], ALU.add).then_inc(g["att"], 1)
                        dve.wait_ge(g["att"], i + 2)
                        link(nc.vector.tensor_scalar(gC[:, :], gA[:, :], 0.0, NEG_INF, ALU.is_equal, ALU.mult))
                        link(nc.vector.tensor_tensor(gB[:, :], gB[:, :], gC[:, :], ALU.add))
                        nc.vector.tensor_reduce(gmx[:, 1:2], gB[:, :], AX.X, ALU.max, negate=True).then_inc(g["mx"], 1)
                        dve.wait_ge(g["ex"], i + 1)
                        link(nc.vector.reciprocal(gmx[:, 3:4], gmx[:, 2:3]))
                        nc.vector.scalar_tensor_tensor(gB[:, :], gB[:, :], gmx[:, 3:4], gA[:, :], ALU.mult, ALU.mult).then_inc(g["w"], 1)
                with dve.Fori(0, NG) as G:
                    cand_dve(dve, gf, G * 2, SC2)
                    dve.wait_ge(gx_in, 16 * (G + 1))
                    new_dve(dve, gf, G * 2, SC2, xg[0][:, :], ST[:, bass.ds(G * GP, GP)])
                    cand_dve(dve, gf, G * 2 + 1, SC2)
                    new_dve(dve, gf, G * 2 + 1, SC2, xg[0][:, :], gs)
                    sum_dve(dve, gy, G, G, gs, (gf["new"], G * 2 + 4))
                    y_dve(dve, gy, G, G)
                    norm_dve(dve, gy, G)

            rest(dve, general)

        @block.scalar
        def _(act):
            act.sem_inc(g["ev"], 1)
            act.sem_inc(g["cp"], 1)
            act.sem_inc(g["nev"], 1)
            act.sem_inc(g["sev"], 1)
            act.sem_inc(signs_counted, 4)
            act.sem_inc(sums_read, 2)
            act.sem_inc(heads_read, 2)
            act.sem_inc(spread_by_act, 2)

            def count_signs(t, r):
                act.wait_ge(signs_counted, t + 4)
                nc.scalar.activation(junk, A[r], ACT.Sign, accum_out=sgn[:, bass.ds(t, 1), 0:1].rearrange("p a b -> p (a b)")).then_inc(signs_half, 1)
                act.wait_ge(signs_half, t + 1)
                nc.scalar.activation(junk, A[r], ACT.Relu, scale=-1.0, accum_out=sgn[:, bass.ds(t, 1), 1:2].rearrange("p a b -> p (a b)")).then_inc(signs_counted, 1)

            def weigh(G, par):
                for r in range(GT - 1):
                    act.wait_ge(ones_made, G * GT + r + 1)
                    for c in range(KC):
                        last = nc.scalar.activation(D1[r][:, c, 0, :], D1[r][:, c, 1, :], ACT.Copy, scale=vQ[par][:, r * KC + c:r * KC + c + 1])
                    last.then_inc(weighed, 1)

            def evict(t, r):
                act.wait_ge(sums_done, t + 9)
                nc.scalar.activation(ST[:, bass.ds(t * P, P)], B[r % 2][:, 0:P], ACT.Copy)
                nc.scalar.activation(HS[:, r % 2, :], B[r % 2][:, P:2 * P], ACT.Copy).then_inc(sums_read, 1)

            def step1(G, par, edge, ahead):
                weigh(G, par)
                if edge:
                    gates_act(act, fe, G - 1, 0, SC1, True)
                for r in range(GT):
                    t = G * GT + r
                    if ahead:
                        act.wait_ge(a_in[r], 16 * (G + 2))
                        count_signs(t + GT, r)
                    evict(t, r)
                    if edge and r == 0:
                        cand_act(act, fe, G - 1, 0, SC1, True)

            for r in range(GT):
                act.wait_ge(a_in[r], 16)
                count_signs(r, r)
            act.wait_ge(u_made, 1)
            for k, o in ((0, 0), (3, 3), (6, 3), (9, 0)):
                last = nc.scalar.activation(U[:, k:k + 3], B[2][:, o:o + 3], ACT.Copy)
            last.then_inc(u_copied, 1)
            act.wait_ge(constants_made, 4)
            act.wait_ge(gate_biases, 7)
            step1(0, 0, False, True)
            with act.Fori(0, NG // 2 - 2) as it:
                step1(it * 2 + 1, 1, True, True)
                step1(it * 2 + 2, 0, True, True)
            step1(NG - 3, 1, True, True)
            step1(NG - 2, 0, False, True)
            step1(NG - 1, 1, False, False)
            for n in range(NG - 3, NG):
                gates_act(act, fe, n, 0, SC1, True)
                cand_act(act, fe, n, 0, SC1, True)

            def spread(t, r, par, first=1):
                act.wait_ge(ones2_made, t + 1)
                for c in range(KC):
                    for h in range(first, HEADS):
                        last = nc.scalar.activation(D2[r][:, c, h, :], OH2[r % 2][:, c, :], ACT.Copy, scale=WQ[par][:, r, c, h:h + 1])
                last.then_inc(spread_by_act, 1)

            def evict2(t, r):
                act.wait_ge(heads_done, t + 9)
                nc.scalar.activation(NS[:, :, r * P:(r + 1) * P], B[r % 2][:, 0:G3].rearrange("p (h i) -> p h i", h=HEADS), ACT.Copy).then_inc(heads_read, 1)

            def mean_heads(G):
                act.wait_ge(w_product, G + 1)
                nc.scalar.activation(SN, B[2][:, :], ACT.Copy, scale=1.0 / HEADS).then_inc(mean_copied, 1)

            def exp(G):
                act.wait_ge(exp_turn, 2 * G + 1)
                nc.scalar.activation(ER[:, :, :], ER[:, :, :], ACT.Exp).then_inc(exp_turn, 1)

            def step2(G, par, before, node, ahead):
                t = G * GT
                if before:
                    evict2(t - 2, 2)
                spread(t, 0, par)
                if before:
                    evict2(t - 1, 3)
                if node:
                    cand_act(act, fn, G - 2, 1, SC2)
                spread(t + 1, 1, par)
                if before:
                    mean_heads(G - 1)
                evict2(t, 0)
                spread(t + 2, 2, par)
                if ahead:
                    exp(G + 1)
                evict2(t + 1, 1)
                spread(t + 3, 3, par)
                if node:
                    dev_act(act, y, G - 2)
                if before:
                    gates_act(act, fn, G - 1, 1, SC2)

            exp(0)
            step2(0, 0, False, False, True)
            step2(1, 1, True, False, True)
            with act.Fori(1, NG // 2 - 1) as it:
                step2(it * 2, 0, True, True, True)
                step2(it * 2 + 1, 1, True, True, True)
            step2(NG - 2, 0, True, True, True)
            t = T - GT
            evict2(t - 2, 2)
            evict2(t - 1, 3)
            mean_heads(NG - 2)
            spread(t, 0, 1, 2)
            cand_act(act, fn, NG - 3, 1, SC2)
            spread(t + 1, 1, 1, 2)
            evict2(t, 0)
            spread(t + 2, 2, 1, 2)
            gates_act(act, fn, NG - 2, 1, SC2)
            evict2(t + 1, 1)
            spread(t + 3, 3, 1, 2)
            dev_act(act, y, NG - 3)
            cand_act(act, fn, NG - 2, 1, SC2)
            evict2(t + 2, 2)
            evict2(t + 3, 3)
            mean_heads(NG - 1)
            dev_act(act, y, NG - 2)
            gates_act(act, fn, NG - 1, 1, SC2)
            cand_act(act, fn, NG - 1, 1, SC2)
            dev_act(act, y, NG - 1)

            def general():
                with act.Fori(0, T) as t:
                    act.wait_ge(g["mm"], t + 2)
                    nc.scalar.activation(ST[:, bass.ds(t * P, P)], B[0][:, 0:P], ACT.Copy)
                    nc.scalar.activation(gH[:, :], B[0][:, P:G3], ACT.Copy).then_inc(g["ev"], 1)
                with act.Fori(0, T) as t:
                    for h in range(HEADS):
                        i = t * HEADS + h
                        act.wait_ge(g["mx"], i + 1)
                        nc.scalar.activation(gB[:, :], gB[:, :], ACT.Exp, bias=gmx[:, 1:2], accum_out=gmx[:, 2:3]).then_inc(g["ex"], 1)
                        for q in range(8):
                            act.wait_ge(g["tr"], 8 * i + q + 2)
                            nc.scalar.activation(gW[:, q * 512:(q + 1) * 512], B[q % 2][:, :], ACT.Copy).then_inc(g["cp"], 1)
                        act.wait_ge(g["num"], i + 1)
                        nc.scalar.activation(gN[:, h, :], B[2][:, 0:P], ACT.Copy).then_inc(g["nev"], 1)
                    act.wait_ge(g["sup"], t + 1)
                    nc.scalar.activation(NST[:, bass.ds(t * P, P)], B[3][:, 0:P], ACT.Copy, scale=1.0 / HEADS).then_inc(g["sev"], 1)
                with act.Fori(0, NG) as G:
                    for k in range(2):
                        gates_act(act, gf, G * 2 + k, k, SC2)
                        cand_act(act, gf, G * 2 + k, k, SC2)
                    dev_act(act, gy, G)

            rest(act, general)

        @block.tensor
        def _(pe):
            pe.sem_inc(g["mm"], 1)
            pe.sem_inc(sums_done, 8)
            pe.sem_inc(heads_done, 8)
            pe.sem_inc(g["tr"], 1)
            pe.wait_ge(setup_in, LOADS)
            pe.wait_ge(constants_made, 4)
            for h in range(HEADS):
                for k in range(2):
                    last = nc.tensor.matmul(B[2][:, 3 * k + h:3 * k + h + 1], WT[:, h, :], a12[:, 3 * k + h:3 * k + h + 1], start=True, stop=True)
            last.then_inc(u_made, 1)
            pe.wait_ge(u_copied, 1)

            def edge_gates(G, par):
                pe.wait_ge(sums_read, G * GT + GT + 2)
                arrived_x(pe, G, par)
                gates(pe, fe, G, 0, ST[:, bass.ds(G * GP, GP)], xg[par][:, :])

            def sums(G, par, edge, scores=B[2]):
                if edge:
                    edge_gates(G - 1, 1 - par)
                for r in range(GT):
                    t = G * GT + r
                    pe.wait_ge(h_in[r % 2], 16 * KC * (G * 2 + r // 2 + 1))
                    if r < GT - 1:
                        pe.wait_ge(weighed, G * (GT - 1) + r + 1)
                    else:
                        pe.wait_ge(weighed_by_pool, G + 1)
                    pe.wait_ge(sums_read, t + 1)
                    for c in range(KC):
                        last = nc.tensor.matmul(B[r % 2][:, 0:2 * P], HG1[r % 2][:, c, :], D1[r][:, c, :, :].rearrange("p w i -> p (w i)"), start=(c == 0), stop=(c == KC - 1))
                    last.then_inc(sums_done, 1)
                    pe.wait_ge(sums_read, t + 3)
                    nc.tensor.matmul(scores[:, bass.ds(t * HEADS, HEADS)], HS[:, r % 2, :], U[:, 0:HEADS], start=True, stop=True).then_inc(score_sums, 1)

            sums(0, 0, False)
            with pe.Fori(0, NG // 2 - 2) as it:
                sums(it * 2 + 1, 1, True)
                sums(it * 2 + 2, 0, True)
            sums(NG - 3, 1, True)
            sums(NG - 2, 0, False)
            sums(NG - 1, 1, False, B[3])
            pe.wait_ge(check_total, 1)
            pe.wait_ge(scores_done, 2)
            nc.tensor.matmul(B[3][0:1, P:P + 2], ones[:, 0:1], chk[:, 2:4], start=True, stop=True).then_inc(check_total, 1)

            def heads(t, r, rows):
                pe.wait_ge(spread_by_dve, t + 1)
                pe.wait_ge(spread_by_act, t + 3)
                pe.wait_ge(heads_read, t + 1)
                for c in range(KC):
                    last = nc.tensor.matmul(B[r % 2][:, 0:G3], rows(r, c), D2[r][:, c, :, :].rearrange("p h i -> p (h i)"), start=(c == 0), stop=(c == KC - 1))
                last.then_inc(heads_done, 1)

            def times_w(G):
                pe.wait_ge(heads_read, G * GT + GT + 2)
                for h in range(HEADS):
                    last = nc.tensor.matmul(B[2][:, :], W[:, h, :], NS[:, h, :], start=(h == 0), stop=(h == HEADS - 1))
                last.then_inc(w_product, 1)

            def node_gates(G, par):
                pe.wait_ge(mean_copied, G + 1)
                arrived_x(pe, G + NG, par)
                gates(pe, fn, G, 1, SN, xg[par][:, :])

            def step(G, par, before, node):
                rows = lambda r, c: HG2[par][:, r * KC + c, 0:P]
                t = G * GT
                heads(t, 0, rows)
                if before:
                    times_w(G - 1)
                heads(t + 1, 1, rows)
                if node:
                    back_pe(pe, y, G - 2)
                if before:
                    node_gates(G - 1, 1 - par)
                heads(t + 2, 2, rows)
                heads(t + 3, 3, rows)

            edge_gates(NG - 3, 1)
            edge_gates(NG - 2, 0)
            edge_gates(NG - 1, 1)
            pe.wait_ge(flag_set, 1)
            step(0, 0, False, False)
            pe.wait_ge(fe["pre"], NG + 1)
            step(1, 1, True, False)
            with pe.Fori(1, NG // 2 - 1) as it:
                step(it * 2, 0, True, True)
                step(it * 2 + 1, 1, True, True)
            step(NG - 2, 0, True, True)
            times_w(NG - 2)
            node_gates(NG - 2, 0)
            for r in range(GT):
                heads(T - GT + r, r, lambda r, c: HG2[1][:, r * KC + c, 0:P])
                if r == 1:
                    back_pe(pe, y, NG - 3)
            times_w(NG - 1)
            back_pe(pe, y, NG - 2)
            node_gates(NG - 1, 1)
            back_pe(pe, y, NG - 1)

            def general():
                pe.wait_ge(g["ld"], 16)
                with pe.Fori(0, T) as t:
                    pe.wait_ge(g["pm"], t + 1)
                    pe.wait_ge(g["ev"], t + 1)
                    for k, src in enumerate((gA, gB, gC)):
                        for j in range(T):
                            last = nc.tensor.matmul(B[0][:, k * P:(k + 1) * P], X[:, j, :], src[:, j * P:(j + 1) * P], start=(j == 0), stop=(j == T - 1))
                    last.then_inc(g["mm"], 1)
                    pe.wait_ge(g["ev"], t + 2)
                    pe.wait_ge(g["ed"], t + 1)
                    nc.tensor.matmul(B[4][:, 0:6], gH[:, 0:P], U[:, 0:6], start=True, stop=False)
                    nc.tensor.matmul(B[4][:, 0:6], gH[:, P:], U[:, 6:12], start=False, stop=True).then_inc(g["e"], 1)
                with pe.Fori(0, T) as t:
                    for h in range(HEADS):
                        i = t * HEADS + h
                        pe.wait_ge(g["w"], i + 2)
                        for q in range(8):
                            if q < 2:
                                pe.wait_ge(g["cp"], 8 * i + 1)
                            else:
                                pe.wait_ge(g["cp"], 8 * i + q)
                            for j in range(4):
                                last = nc.tensor.transpose(B[q % 2][:, j * P:(j + 1) * P], gB[:, (4 * q + j) * P:(4 * q + j + 1) * P], ident[:, :])
                            last.then_inc(g["tr"], 1)
                        pe.wait_ge(g["cp"], 8 * i + 8 + 1)
                        pe.wait_ge(g["nev"], i + 1)
                        for j in range(T):
                            last = nc.tensor.matmul(B[2][:, 0:P], X[:, j, :], gW[:, j * P:(j + 1) * P], start=(j == 0), stop=(j == T - 1))
                        last.then_inc(g["num"], 1)
                    pe.wait_ge(g["nev"], (t + 1) * HEADS + 1)
                    pe.wait_ge(g["sev"], t + 1)
                    for h in range(HEADS):
                        last = nc.tensor.matmul(B[3][:, 0:P], W[:, h, :], gN[:, h, :], start=(h == 0), stop=(h == HEADS - 1))
                    last.then_inc(g["sup"], 1)
                with pe.Fori(0, NG) as G:
                    pe.wait_ge(g["sev"], T + 1)
                    pe.wait_ge(gx_in, 16 * (G + 1))
                    for k, src in enumerate((ST, NST)):
                        gates(pe, gf, G * 2 + k, k, src[:, bass.ds(G * GP, GP)], xg[0][:, :])
                    back_pe(pe, gy, G)

            rest(pe, general)


def kernel(x, adj, L0_gnn_gat_W, L0_gnn_gat_a, L0_gnn_edge_Wih, L0_gnn_edge_Whh, L0_gnn_edge_bih, L0_gnn_edge_bhh,
           L0_gnn_node_Wih, L0_gnn_node_Whh, L0_gnn_node_bih, L0_gnn_node_bhh):
    import concourse.bacc as _bacc
    from concourse.bass_utils import run_bass_kernel_spmd as _run

    c = np.ascontiguousarray
    x, adj = np.asarray(x), np.asarray(adj)
    w, a = np.asarray(L0_gnn_gat_W), np.asarray(L0_gnn_gat_a)
    side = lambda e, n: c(np.stack([np.asarray(e).T, np.asarray(n).T], axis=1))
    quad = np.arange(P, dtype=np.float32)[:, None]
    arrays = {
        "x1": np.concatenate([np.zeros((1, P), np.float32), x]), "xT": c(x.T), "adj": c(adj), "adjT": c(adj.T),
        "diag": c(np.diagonal(adj).reshape(T, P).T),
        "gatW": c(w.transpose(1, 0, 2)), "gatWT": c(w.transpose(2, 0, 1)),
        "a12": c(a.reshape(HEADS, 2, P).transpose(2, 1, 0).reshape(P, 2 * HEADS)),
        "Wi": side(L0_gnn_edge_Wih, L0_gnn_node_Wih), "Wh": side(L0_gnn_edge_Whh, L0_gnn_node_Whh),
        "b": c(np.stack([np.asarray(v).reshape(3, P).T for v in (L0_gnn_edge_bih, L0_gnn_edge_bhh, L0_gnn_node_bih, L0_gnn_node_bhh)], axis=1)),
        "ident": np.eye(P, dtype=np.float32), "off": 1 - np.eye(P, dtype=np.float32),
        "iota": np.tile(np.arange(P, dtype=np.float32), (P, 1)),
        "rq": quad % Q,
        "bounds": np.tile(np.stack([np.arange(4), np.arange(1, 5)]).astype(np.float32) * N, (P, 1, 1)),
        "seg1": np.tile(np.repeat(np.arange(4, dtype=np.float32) * SEG + 1, 8), (P, GT)) + quad // Q * N,
        "dkey": np.arange(1, N + 1, dtype=np.float32).reshape(T, P).T + quad // Q * N,
    }
    nc = _bacc.Bacc("TRN2", target_bir_lowering=False, num_devices=1)
    d = {k: nc.dram_tensor("in_" + k, v.shape, mybir.dt.from_np(v.dtype), kind="ExternalInput").ap() for k, v in arrays.items()}
    out = nc.dram_tensor("out", (N, P), fp32, kind="ExternalOutput").ap()
    build(nc, d, out)
    r = _run(nc, [{"in_" + k: v for k, v in arrays.items()}], core_ids=[0])
    return r.results[0]["out"]
```
